# Optimizing a Trainium2 kernel written in Bass

```python
import numpy as np
import jax
import jax.numpy as jnp

def _softmax(x, axis=-1):
    return jax.nn.softmax(x, axis=axis)

def _gelu(x):
    return jax.nn.gelu(x, approximate=True)

def _silu(x):
    return jax.nn.silu(x)

def _sigmoid(x):
    return jax.nn.sigmoid(x)

def _layernorm(x, axis=-1, eps=1e-05):
    m = jnp.mean(x, axis=axis, keepdims=True)
    v = jnp.var(x, axis=axis, keepdims=True)
    return (x - m) / jnp.sqrt(v + eps)

def _scatter_add(tgt, idx, src, axis=0):
    return tgt.at[idx].add(src)

def _segment_sum(src, seg, n):
    return jax.ops.segment_sum(src, seg, n)
kernel_name = 'mk_seq_preln_d1_jaxref_r4_361096'

def setup_inputs(seed: int=0):
    np.random.seed(seed)
    _w = jnp.asarray

    def _L0_attn_setup():
        import jax, jax.numpy as jnp
        import numpy as np
        import math
        B, S, D = (2, 512, 512)
        H, KVH = (16, 8)
        Dh = D // H // 2
        GROUPS = H // KVH
        LAYER_IDX = 2
        LAMBDA_INIT = 0.8 - 0.6 * math.exp(-0.3 * LAYER_IDX)
        EPS = 1e-05
        ROPE_THETA = 10000.0

        def _rope_cos_sin(seq_len):
            inv_freq = ROPE_THETA ** (-jnp.arange(Dh, dtype=jnp.float32) / Dh)
            freqs = jnp.arange(seq_len, dtype=jnp.float32)[:, None] * inv_freq[None, :]
            return (jnp.cos(freqs), jnp.sin(freqs))

        def _rotate_half(x):
            x1, x2 = jnp.split(x, 2, axis=-1)
            return jnp.concatenate([-x2, x1], axis=-1)

        def _apply_rope(x, cos, sin):
            return x * cos[None, None] + _rotate_half(x) * sin[None, None]
        key = jax.random.key(seed)
        ks = jax.random.split(key, 9)
        sc = lambda fan_in: 1.0 / np.sqrt(fan_in)
        return {'hidden_states': jax.random.normal(ks[0], (B, S, D), jnp.float32), 'Wq': jax.random.normal(ks[1], (D, D), jnp.float32) * sc(D), 'Wk': jax.random.normal(ks[2], (D // GROUPS, D), jnp.float32) * sc(D), 'Wv': jax.random.normal(ks[3], (D // GROUPS, D), jnp.float32) * sc(D), 'Wo': jax.random.normal(ks[4], (D, D), jnp.float32) * sc(D), 'lambda_q1': jax.random.normal(ks[5], (Dh,), jnp.float32) * 0.1, 'lambda_k1': jax.random.normal(ks[6], (Dh,), jnp.float32) * 0.1, 'lambda_q2': jax.random.normal(ks[7], (Dh,), jnp.float32) * 0.1, 'lambda_k2': jax.random.normal(ks[8], (Dh,), jnp.float32) * 0.1, 'subln_weight': jnp.ones((2 * Dh,), jnp.float32)}
    _L0_attn_in = _L0_attn_setup()

    def _L0_ffn_setup():
        import jax, jax.numpy as jnp
        import numpy as np
        D_MODEL = 512
        D_FF = 2048

        def absmean_quant(w):
            scale = jnp.mean(jnp.abs(w))
            mask = (jnp.abs(w) >= scale * 0.7).astype(w.dtype)
            return jnp.sign(w) * mask
        key = jax.random.key(seed)
        k_x, k_w1, k_w2 = jax.random.split(key, 3)
        x = jax.random.normal(k_x, (4, 1024, D_MODEL), dtype=jnp.float32)
        w1 = jax.random.normal(k_w1, (D_FF, D_MODEL), dtype=jnp.float32)
        b1 = jnp.zeros((D_FF,), dtype=jnp.float32)
        w2 = jax.random.normal(k_w2, (D_MODEL, D_FF), dtype=jnp.float32)
        b2 = jnp.zeros((D_MODEL,), dtype=jnp.float32)
        return {'x': x, 'w1': w1, 'b1': b1, 'w2': w2, 'b2': b2}
    _L0_ffn_in = _L0_ffn_setup()
    _d = {'L0_attn_hidden_states': _L0_attn_in['hidden_states'], 'L0_attn_Wq': _L0_attn_in['Wq'], 'L0_attn_Wk': _L0_attn_in['Wk'], 'L0_attn_Wv': _L0_attn_in['Wv'], 'L0_attn_Wo': _L0_attn_in['Wo'], 'L0_attn_lambda_q1': _L0_attn_in['lambda_q1'], 'L0_attn_lambda_k1': _L0_attn_in['lambda_k1'], 'L0_attn_lambda_q2': _L0_attn_in['lambda_q2'], 'L0_attn_lambda_k2': _L0_attn_in['lambda_k2'], 'L0_attn_subln_weight': _L0_attn_in['subln_weight'], 'L0_ffn_w1': _L0_ffn_in['w1'], 'L0_ffn_b1': _L0_ffn_in['b1'], 'L0_ffn_w2': _L0_ffn_in['w2'], 'L0_ffn_b2': _L0_ffn_in['b2']}
    _x0 = _d['L0_attn_hidden_states']
    _d['L0_attn_hidden_states'] = jax.random.normal(jax.random.fold_in(jax.random.key(seed), 1), (8, 1024, 512), dtype=_x0.dtype)
    del _x0
    return _d

def reference(L0_attn_hidden_states, L0_attn_Wq, L0_attn_Wk, L0_attn_Wv, L0_attn_Wo, L0_attn_lambda_q1, L0_attn_lambda_k1, L0_attn_lambda_q2, L0_attn_lambda_k2, L0_attn_subln_weight, L0_ffn_w1, L0_ffn_b1, L0_ffn_w2, L0_ffn_b2):

    def _L0_attn_ref(hidden_states, Wq, Wk, Wv, Wo, lambda_q1, lambda_k1, lambda_q2, lambda_k2, subln_weight):
        import jax, jax.numpy as jnp
        import numpy as np
        import math
        B, S, D = (2, 512, 512)
        H, KVH = (16, 8)
        Dh = D // H // 2
        GROUPS = H // KVH
        LAYER_IDX = 2
        LAMBDA_INIT = 0.8 - 0.6 * math.exp(-0.3 * LAYER_IDX)
        EPS = 1e-05
        ROPE_THETA = 10000.0

        def _rope_cos_sin(seq_len):
            inv_freq = ROPE_THETA ** (-jnp.arange(Dh, dtype=jnp.float32) / Dh)
            freqs = jnp.arange(seq_len, dtype=jnp.float32)[:, None] * inv_freq[None, :]
            return (jnp.cos(freqs), jnp.sin(freqs))

        def _rotate_half(x):
            x1, x2 = jnp.split(x, 2, axis=-1)
            return jnp.concatenate([-x2, x1], axis=-1)

        def _apply_rope(x, cos, sin):
            return x * cos[None, None] + _rotate_half(x) * sin[None, None]
        bsz, tgt_len, _ = hidden_states.shape
        scaling = Dh ** (-0.5)
        q = hidden_states @ Wq.T
        k = hidden_states @ Wk.T
        v = hidden_states @ Wv.T
        q = q.reshape(bsz, tgt_len, 2 * H, Dh).transpose(0, 2, 1, 3)
        k = k.reshape(bsz, tgt_len, 2 * KVH, Dh).transpose(0, 2, 1, 3)
        v = v.reshape(bsz, tgt_len, KVH, 2 * Dh).transpose(0, 2, 1, 3)
        cos, sin = _rope_cos_sin(tgt_len)
        q = _apply_rope(q, cos, sin)
        k = _apply_rope(k, cos, sin)
        k = jnp.repeat(k, GROUPS, axis=1)
        v = jnp.repeat(v, GROUPS, axis=1)
        q = q * scaling
        scores = jnp.einsum('bhqd,bhkd->bhqk', q, k)
        causal = jnp.triu(jnp.full((tgt_len, tgt_len), -jnp.inf, jnp.float32), k=1)
        scores = scores + causal[None, None]
        probs = jax.nn.softmax(scores.astype(jnp.float32), axis=-1).astype(scores.dtype)
        lambda_1 = jnp.exp(jnp.sum(lambda_q1 * lambda_k1))
        lambda_2 = jnp.exp(jnp.sum(lambda_q2 * lambda_k2))
        lambda_full = lambda_1 - lambda_2 + LAMBDA_INIT
        probs = probs.reshape(bsz, H, 2, tgt_len, tgt_len)
        diff = probs[:, :, 0] - lambda_full * probs[:, :, 1]
        attn = jnp.einsum('bhqk,bhkd->bhqd', diff, v)
        var = jnp.mean(attn.astype(jnp.float32) ** 2, axis=-1, keepdims=True)
        attn = (attn * jax.lax.rsqrt(var + EPS)).astype(attn.dtype) * subln_weight
        attn = attn * (1.0 - LAMBDA_INIT)
        attn = attn.transpose(0, 2, 1, 3).reshape(bsz, tgt_len, H * 2 * Dh)
        return attn @ Wo.T

    def _L0_ffn_ref(x, w1, b1, w2, b2):
        import jax, jax.numpy as jnp
        import numpy as np
        D_MODEL = 512
        D_FF = 2048

        def absmean_quant(w):
            scale = jnp.mean(jnp.abs(w))
            mask = (jnp.abs(w) >= scale * 0.7).astype(w.dtype)
            return jnp.sign(w) * mask
        w1_q = absmean_quant(w1)
        w2_q = absmean_quant(w2)
        h = jnp.einsum('bsd,fd->bsf', x, w1_q) + b1
        h = jax.nn.gelu(h, approximate=False)
        out = jnp.einsum('bsf,df->bsd', h, w2_q) + b2
        return out
    x = L0_attn_hidden_states
    x = x + _L0_attn_ref(_layernorm(x, axis=-1), L0_attn_Wq, L0_attn_Wk, L0_attn_Wv, L0_attn_Wo, L0_attn_lambda_q1, L0_attn_lambda_k1, L0_attn_lambda_q2, L0_attn_lambda_k2, L0_attn_subln_weight)
    x = x + _L0_ffn_ref(_layernorm(x, axis=-1), L0_ffn_w1, L0_ffn_b1, L0_ffn_w2, L0_ffn_b2)
    return x

_drawn_inputs = setup_inputs


def setup_inputs(seed=0):
    import zlib

    import numpy as np

    out = dict(_drawn_inputs(seed))
    spreads = {'L0_attn_subln_weight': (1.0, 0.2), 'L0_ffn_b1': (0.0, 0.8), 'L0_ffn_b2': (0.0, 0.8)}
    factors = {'L0_attn_lambda_q1': 8.0, 'L0_attn_lambda_q2': 5.83, 'L0_attn_lambda_k2': 3.621}
    for name, (base, spread) in spreads.items():
        noise = np.random.default_rng([zlib.crc32(name.encode()), seed]).standard_normal(out[name].shape)
        drawn = base * np.exp(spread * noise) if base else spread * noise
        out[name] = jnp.asarray(drawn.astype(out[name].dtype))
    for name, factor in factors.items():
        out[name] = (out[name] * factor).astype(out[name].dtype)
    return out
```

```python
import math
from contextlib import ExitStack

import numpy as np

import concourse.bass as bass
from concourse import mybir

F32 = mybir.dt.float32
F16 = mybir.dt.float16
BF16 = mybir.dt.bfloat16
F8 = mybir.dt.float8e4
ALU = mybir.AluOpType
ACT = mybir.ActivationFunctionType
AX = mybir.AxisListType

P = 128
B, S, D = 8, 1024, 512
H, KVH = 16, 8
DH = D // H // 2
DV = 2 * DH
NQ, NK = 2 * H, 2 * KVH
DKV = NK * DH
FF = 2048
KD = D // P
FT = FF // P
TILES = S // P
HALF = H // 2
EPS = 1e-5
LAMBDA_INIT = 0.8 - 0.6 * math.exp(-0.3 * 2)
ROPE_THETA = 10000.0
TERNARY_CUT = 0.7
MASKED = -1e30
XS = 2048.0
HS = 1.0 / 16
PROD = 6
QPART = (0, 0, 0, 1, 1, 2)
KPART = (0, 1, 2, 0, 1, 0)
ROWS = PROD * DH
LAG = 2
GELU_F = FT // 2



def groups(i):
    return 1 if i < 4 else 2


def tg(i, n, g):
    return (H * i if i < 4 else H * 4 + 2 * H * (i - 4)) + n * groups(i) + g


def pg(i, u, g):
    return (2 * i if i < 4 else 8 + 4 * (i - 4)) + u * groups(i) + g


def banks(i, s):
    return [s % 4] if i < 4 else [2 * (s % 2), 2 * (s % 2) + 1]


def slot_users():
    last, need = {}, []
    for i in range(TILES):
        for s in range(NQ):
            need.append(max([last.get(k, 0) for k in banks(i, s)]))
            for k in banks(i, s):
                last[k] = i * NQ + s + 1
    return need


SLOT_FREE = slot_users()
N_T = tg(TILES - 1, H - 1, 1) + 1
N_PV = pg(TILES - 1, 1, 1) + 1


def diff_attention_ffn(nc, x, wqT, wkT, wvT, woT, lams, subw, w1T, b1, w2T, b2, rope, out):
    ctx = ExitStack()
    with ctx:
        def sb(name, shape, dt):
            return ctx.enter_context(nc.sbuf_tensor(name, shape, dt))

        def sem(name):
            return ctx.enter_context(nc.semaphore(name))

        WQKV = sb("WQKV", [P, KD, D + 2 * DKV], F32)
        WO = sb("WO", [P, KD, D], F32)
        W1Q = sb("W1Q", [P, KD, FF], F8)
        W2Q = sb("W2Q", [P, FT, D], F8)
        ident = sb("ident", [P, P], F32)
        identb = sb("identb", [P, P], BF16)
        maskb = sb("maskb", [P, P], BF16)
        onesf = sb("onesf", [P, P], F32)
        nhalf = sb("nhalf", [P, H], F32)
        ropet = sb("ropet", [P, 2, TILES, DH], F32)
        b1c = sb("b1c", [P, FT], F32)
        b2b = sb("b2b", [P, D], F32)
        subc = sb("subc", [P, 1], F32)
        lamt = sb("lamt", [P, 4, DH], F32)
        lamp = sb("lamp", [P, 2, DH], F32)
        lams2 = sb("lams2", [P, 2], F32)
        lame = sb("lame", [P, 2], F32)
        neglam = sb("neglam", [P, 1], F32)
        wsum = sb("wsum", [P, 2, 64], F32)
        wtot = sb("wtot", [P, 2], F32)
        thr = sb("thr", [P, 2, 2], F32)
        KST = sb("KST", [P, TILES, NK, P], BF16)
        QST = sb("QST", [P, 2, NQ, P], BF16)
        V = sb("V", [P, TILES, DKV], F32)
        E1 = sb("E1", [P, 2, S], F32)
        E2 = sb("E2", [P, S], F32)
        DT = sb("DT", [P, TILES, HALF, P], F32)
        NM = sb("NM", [P, 8], F32)
        SUM = sb("SUM", [P, 2, 2, H], F32)
        RS = sb("RS", [P, 2, 2, H], F32)
        CC = sb("CC", [P, 2], F32)
        X = sb("X", [P, 4, D], F32)
        TOK = sb("TOK", [P, D], F32)
        WT = sb("WT", [P, D], F32)
        ST = sb("ST", [P, 6], F32)
        MV = sb("MV", [P, 2], F32)
        VE = sb("VE", [P, H], F32)
        RST = sb("RST", [P, H], F32)
        T1 = sb("T1", [P, D + DKV], F32)
        T2 = sb("T2", [P, D + DKV], F32)
        SPL = sb("SPL", [P, 3, D + DKV], BF16)
        AT = sb("AT", [P, D], F32)
        SQ = AT
        MS = sb("MS", [P, H], F32)
        X1 = sb("X1", [P, 4, D], F32)
        X2H = sb("X2H", [P, KD, 2 * P], F16)
        X2L = sb("X2L", [P, KD, 2 * P], F16)
        HP = sb("HP", [P, GELU_F, 2 * P], F32)
        HH = sb("HH", [P, FT, 2 * P], F16)
        HL = sb("HL", [P, FT, 2 * P], F16)
        OUT = AT

        SP_ = ctx.enter_context(nc.psum_tensor("SP_", [P, 4, 512], F32))
        DP = ctx.enter_context(nc.psum_tensor("DP", [P, 512], F32))
        PV = ctx.enter_context(nc.psum_tensor("PV", [P, 512], F32))
        M = ctx.enter_context(nc.psum_tensor("M", [P, 512], F32))
        F = ctx.enter_context(nc.psum_tensor("F", [P, 512], F32))

        scratch = nc.dram_tensor("scratch", [2, P, 3, D + DKV], BF16, kind="Internal").ap()

        w_in = sem("w_in")
        w1_in = sem("w1_in")
        w2_in = sem("w2_in")
        pool_const = sem("pool_const")
        lam_prod = sem("lam_prod")
        lam_exp = sem("lam_exp")
        set_chain = sem("set_chain")
        abs_sum = sem("abs_sum")
        abs_all = sem("abs_all")
        ready = sem("ready")
        x_in = [sem("x_in_even"), sem("x_in_odd")]
        ln_var = sem("ln_var")
        ln_rstd = sem("ln_rstd")
        ln_chain = sem("ln_chain")
        xn_ready = sem("xn_ready")
        m_xt = sem("m_xt")
        xt_ready = sem("xt_ready")
        m_q = sem("m_q")
        q_roped = sem("q_roped")
        m_kv = sem("m_kv")
        kv_roped = sem("kv_roped")
        rope_sum = sem("rope_sum")
        m_qt = sem("m_qt")
        m_kt = sem("m_kt")
        high_part = sem("high_part")
        rest_part = sem("rest_part")
        mid_part = sem("mid_part")
        split_done = sem("split_done")
        scr_out = sem("scr_out")
        stacked = sem("stacked")
        s_ready = sem("s_ready")
        max_ready = sem("max_ready")
        exp_done = sem("exp_done")
        d_chain = sem("d_chain")
        d_ready = sem("d_ready")
        t_ready = sem("t_ready")
        dt_ready = sem("dt_ready")
        pv_done = sem("pv_done")
        at_ready = sem("at_ready")
        m_at = sem("m_at")
        attn_ready = sem("attn_ready")
        sq_ready = sem("sq_ready")
        ms_chain = sem("ms_chain")
        ms_ready = sem("ms_ready")
        rms_ready = sem("rms_ready")
        an_ready = sem("an_ready")
        m_ant = sem("m_ant")
        ant_ready = sem("ant_ready")
        m_wo = sem("m_wo")
        x1_ready = sem("x1_ready")
        xn2_ready = sem("xn2_ready")
        m_x2t = sem("m_x2t")
        x2h_ready = sem("x2h_ready")
        x2_ready = sem("x2_ready")
        f1_ready = sem("f1_ready")
        hp_ready = sem("hp_ready")
        gelu_done = sem("gelu_done")
        h_chain = sem("h_chain")
        h_ready = sem("h_ready")
        f2_ready = sem("f2_ready")
        o_sum = sem("o_sum")
        o_ready = sem("o_ready")
        o_out = sem("o_out")
        held = sem("held")

        w1f = DT[:, :, :, :].rearrange("p a b c -> p (a b c)")
        w2f = KST[:, :, :, :].rearrange("p a b c -> p (a b c)").bitcast(F32)
        cutt = HP[:, :, :].rearrange("p a b -> p (a b)")

        def hold(eng, signal, value):
            if not isinstance(value, int) or value > 0:
                eng.wait_ge(signal, value)
                eng.sem_inc(held, 1)

        def after(eng, signal, value):
            if not isinstance(value, int) or value > 0:
                eng.wait_ge(signal, value)

        def score_out(i, s, w):
            k = banks(i, s)
            return SP_[:, k[0]:k[0] + len(k), :].rearrange("p a b -> p (a b)")[:, 0:w]

        def qk3(ap):
            return ap.rearrange("p (s d) -> p s d", d=DH)

        def next_tile(t):
            return None if t in (7, 9) else (t + 1) % 9 if t < 8 else 0

        def built(b, t):
            return b * TILES + (t + 1 if t < 8 else TILES)

        block = ctx.enter_context(nc.Block())

        @block.sync
        def _(sp):
            sp.dma_start(w1f.rearrange("p (k n) -> p k n", k=KD), w1T.rearrange("(k p) n -> p k n", p=P)).then_inc(w1_in, 16)
            sp.dma_start(w2f.rearrange("p (k n) -> p k n", k=FT), w2T.rearrange("(k p) n -> p k n", p=P)).then_inc(w2_in, 16)
            for j in range(2):
                sp.dma_start(X[:, j, :], x[0, j * P:(j + 1) * P, :]).then_inc(x_in[j], 16)
            sp.dma_start(WQKV[:, :, 0:D], wqT.rearrange("(k p) n -> p k n", p=P)).then_inc(w_in, 16)
            sp.dma_start(WQKV[:, :, D:D + DKV], wkT.rearrange("(k p) n -> p k n", p=P)).then_inc(w_in, 16)
            sp.dma_start(WQKV[:, :, D + DKV:D + 2 * DKV], wvT.rearrange("(k p) n -> p k n", p=P)).then_inc(w_in, 16)
            sp.dma_start(WO[:, :, :], woT.rearrange("k p n -> p k n")).then_inc(w_in, 16)
            sp.dma_start(ropet[:, :, :, :], rope).then_inc(w_in, 16)
            sp.dma_start(b1c[:, :], b1).then_inc(w_in, 16)
            sp.dma_start(b2b[:, :], b2.partition_broadcast(P)).then_inc(w_in, 16)
            for j in range(4):
                sp.dma_start(lamt[:, j, :], lams[j].partition_broadcast(P)).then_inc(w_in, 16)
                sp.dma_start(subc[DV * j:DV * (j + 1), :], subw.unsqueeze(1)).then_inc(w_in, 16)

            def stack(b, nb, tile, s_done):
                hold(sp, split_done, 2 * nb + 2)
                sp.dma_start(scratch[tile % 2], SPL[:, :, :]).then_inc(scr_out, 16)
                hold(sp, scr_out, 16 * nb + 16)
                if s_done is not None:
                    hold(sp, s_ready, s_done)
                src = scratch[tile % 2].rearrange("(s d) a (c n) -> a d s c n", d=DH, n=P)
                for j in range(PROD):
                    r = slice(DH * j, DH * (j + 1))
                    sp.dma_start(QST[r, tile % 2, :, :].rearrange("p (s c) n -> p s c n", s=8),
                                 src[QPART[j], :, :, 0:4, :]).then_inc(stacked, 16)
                    sp.dma_start(KST[r, tile, :, :].rearrange("p (s c) n -> p s c n", s=8),
                                 src[KPART[j], :, :, 4:6, :]).then_inc(stacked, 16)

            sp.wait_ge(ready, 5)
            stack(0, 0, 0, None)
            def one_pass(b):
                for t in range(TILES + 2):
                    if t < TILES:
                        j = (t + 2) % TILES
                        hold(sp, x1_ready, b * TILES + max(t - 1, 0))
                        row = x[b] if t < 6 else x[b + 1]
                        sp.dma_start(X[:, j % 4, :], row[j * P:(j + 1) * P, :]).then_inc(x_in[t % 2], 16)
                    if next_tile(t) is not None:
                        done = b * NQ * TILES + NQ * (t if t < 8 else TILES)
                        stack(b, built(b, t), next_tile(t), done)
                    if t in (3, 5, 7, 9):
                        for j in range(2):
                            k = t - 3 + j
                            hold(sp, o_ready, b * TILES + k + 1)
                            sp.dma_start(out[b, k * P:(k + 1) * P, :], OUT[:, :]).then_inc(o_out, 16)

            one_pass(0)
            with sp.Fori(1, B) as b:
                one_pass(b)
            sp.wait_ge(o_out, 16 * B * TILES)

        @block.gpsimd
        def _(pool):
            pool.memset(ident[:, :], 0.0).then_inc(pool_const, 1)
            pool.memset(identb[:, :], 0.0).then_inc(pool_const, 1)
            pool.memset(maskb[:, :], 0.0).then_inc(pool_const, 1)
            pool.memset(onesf[:, :], 1.0).then_inc(pool_const, 1)
            pool.memset(nhalf[:, :], -0.5).then_inc(pool_const, 1)
            pool.wait_ge(pool_const, 5)
            for m in (ident, identb):
                pool.affine_select(out=m[:, :], in_=m[:, :], compare_op=ALU.not_equal, fill=1.0,
                                   base=0, pattern=[[-1, P]], channel_multiplier=1).then_inc(pool_const, 1)
            pool.affine_select(out=maskb[:, :], in_=maskb[:, :], compare_op=ALU.is_ge, fill=MASKED,
                               base=0, pattern=[[-1, P]], channel_multiplier=1).then_inc(pool_const, 1)
            pool.wait_ge(pool_const, 8)

            def rstd(nv):
                after(pool, ln_var, nv + 1)
                pool.tensor_tensor(RST[:, 0:1], VE[:, 0:1], nhalf[:, 0:1], ALU.pow).then_inc(ln_rstd, 1)

            def rope_add(nb, part):
                c = slice(0, D) if part == 0 else slice(D, D + DKV)
                after(pool, q_roped if part == 0 else kv_roped, nb + 1)
                pool.tensor_tensor(T1[:, c], T1[:, c], T2[:, c], ALU.add).then_inc(rope_sum, 1)

            def split(nb, part):
                c = slice(0, D) if part == 0 else slice(D, D + DKV)
                hold(pool, rest_part, 2 * nb + part + 1)
                pool.tensor_scalar(SPL[:, 1, c], T2[:, c], 1.0, 0.0, ALU.mult, ALU.add).then_inc(mid_part, 1)
                after(pool, mid_part, 2 * nb + part + 1)
                pool.tensor_tensor(SPL[:, 2, c], T2[:, c], SPL[:, 1, c], ALU.subtract).then_inc(split_done, 1)

            def hidden_split(b, c, half):
                nh = b * 8 + 2 * c + half
                fs = slice(GELU_F * half, GELU_F * (half + 1))
                after(pool, gelu_done, nh + 1)
                hold(pool, f2_ready, b * TILES + 2 * c)
                pool.tensor_scalar(HH[:, fs, :], HP[:, :, :], HS, 0.0, ALU.mult, ALU.add).then_inc(h_chain, 1)
                hold(pool, h_chain, 2 * nh + 1)
                pool.tensor_scalar(HP[:, :, :], HP[:, :, :], HS, 0.0, ALU.mult, ALU.add).then_inc(h_chain, 1)
                after(pool, h_chain, 2 * nh + 2)
                pool.tensor_tensor(HL[:, fs, :], HP[:, :, :], HH[:, fs, :], ALU.subtract).then_inc(h_ready, 1)

            rstd(0)
            rope_add(0, 0)
            rope_add(0, 1)
            split(0, 0)
            split(0, 1)
            def one_pass(b):
                for t in range(TILES + 2):
                    nb = built(b, t)
                    lt = b * (2 * TILES) + 1 + (2 * t - 1 if t else 0)
                    build = next_tile(t) is not None
                    finish = 1 <= t <= 8
                    if t == 8:
                        lt = b * (2 * TILES) + 2 * TILES - 1
                    if t == 9:
                        lt = b * (2 * TILES) + 2 * TILES + 1
                    for s in range(H):
                        if s == 0 and build:
                            rstd(lt)
                        if s == 3 and build:
                            rope_add(nb, 0)
                        if s == 4 and build:
                            rope_add(nb, 1)
                        if s == 5 and finish:
                            nf = b * TILES + t - 1
                            after(pool, attn_ready, nf + 1)
                            pool.tensor_tensor(SQ[:, :], TOK[:, :], TOK[:, :], ALU.mult).then_inc(sq_ready, 1)
                        if s == 6:
                            if build:
                                split(nb, 0)
                            if finish:
                                after(pool, ms_ready, nf + 1)
                                pool.tensor_tensor(RST[:, :], VE[:, :], nhalf[:, :], ALU.pow).then_inc(rms_ready, 1)
                        if s == 7 and build:
                            split(nb, 1)
                        if s == 10 and finish:
                            rstd(lt + (1 if build else 0))
                        if t in (3, 5, 7, 9):
                            c = (t - 3) // 2
                            if s == 1:
                                hidden_split(b, c, 0)
                            if s == 8:
                                hidden_split(b, c, 1)
                            if s in (12, 15):
                                k = b * TILES + 2 * c + (0 if s == 12 else 1)
                                after(pool, o_sum, k + 1)
                                pool.tensor_tensor(OUT[:, :], OUT[:, :], b2b[:, :], ALU.add).then_inc(o_ready, 1)

            one_pass(0)
            with pool.Fori(1, B) as b:
                one_pass(b)

        @block.scalar
        def _(act):
            act.wait_ge(lam_prod, 1)
            act.activation(lame[:, :], lams2[:, :], ACT.Exp).then_inc(lam_exp, 1)

            def xt_copy(nb, wo_done):
                after(act, m_xt, nb + 1)
                after(act, m_wo, wo_done)
                act.activation(WT[:, :], M[:, :], ACT.Copy).then_inc(xt_ready, 1)

            def high(nb, part):
                c, n = (slice(0, D), D) if part == 0 else (slice(D, D + DKV), DKV)
                after(act, m_qt if part == 0 else m_kt, nb + 1)
                if part == 0:
                    after(act, scr_out, 16 * nb)
                act.activation(SPL[:, 0, c], M[:, 0:n], ACT.Copy).then_inc(high_part, 1)

            def exp(b, i, n, k):
                j = b * NQ * TILES + i * NQ + 2 * n + k
                u = i * H + n
                w = P * (i + 1)
                after(act, max_ready, j + 1)
                if k == 0 and u >= 2:
                    pi, pn = divmod(u - 2, H)
                    after(act, t_ready, b * N_T + tg(pi, pn, groups(pi) - 1) + 1)
                if k == 1:
                    after(act, d_ready, b * H * TILES + u)
                dst = E1[:, u % 2, 0:w] if k == 0 else E2[:, 0:w]
                col = 8 * (n // 8) + 4 * (n % 2) + (n % 8) // 2
                act.activation(dst, score_out(i, 2 * n + k, w), ACT.Exp, bias=NM[:, (2 * u + k) % 8:(2 * u + k) % 8 + 1],
                               scale=1.0, accum_out=SUM[:, i % 2, k, col:col + 1]).then_inc(exp_done, 1)

            def dt_copy(b, i, n, g):
                k0, k1 = 4 * g, min(4 * g + 4, i + 1)
                after(act, t_ready, b * N_T + tg(i, n, g) + 1)
                if n % HALF == 0:
                    if n or i:
                        pi, pu = (i, 0) if n else (i - 1, 1)
                        after(act, pv_done, b * N_PV + pg(pi, pu, min(g, groups(pi) - 1)) + 1)
                act.activation(DT[:, k0:k1, n % HALF, :], DP[:, 0:P * (k1 - k0)].rearrange("p (k q) -> p k q", q=P),
                               ACT.Copy).then_inc(dt_ready, 1)

            xt_copy(0, 0)
            high(0, 0)
            high(0, 1)
            def one_pass(b):
                for t in range(TILES + 2):
                    nb = built(b, t)
                    build = next_tile(t) is not None
                    finish = 1 <= t <= 8
                    nf = b * TILES + t - 1
                    for s in range(H):
                        i, n = (t, s - LAG) if s >= LAG else (t - 1, s - LAG + H)
                        drain = 0 <= i < TILES
                        if drain:
                            dt_copy(b, i, n, 0)
                        if t < TILES:
                            exp(b, t, s, 0)
                        if drain and groups(i) == 2:
                            dt_copy(b, i, n, 1)
                        if t < TILES:
                            exp(b, t, s, 1)
                        if s == 2 and build:
                            xt_copy(nb, b * TILES + (t - 1 if 0 < t else 0))
                        if s == 3 and finish:
                            after(act, pv_done, b * N_PV + pg(t - 1, 1, groups(t - 1) - 1) + 1)
                            after(act, ms_ready, nf)
                            after(act, o_out, 16 * (b * TILES + 2 * ((t - 2) // 2) if t >= 4 else b * TILES))
                            act.activation(AT[:, :], PV[:, :], ACT.Copy).then_inc(at_ready, 1)
                        if s == 6 and build:
                            high(nb, 0)
                        if s == 7 and build:
                            high(nb, 1)
                        if s == 8 and finish:
                            after(act, m_ant, nf + 1)
                            act.activation(WT[:, :], M[:, :], ACT.Copy).then_inc(ant_ready, 1)
                        if s == 12 and finish:
                            after(act, m_x2t, nf + 1)
                            if t % 2:
                                after(act, f1_ready, b * 32 + 8 * ((t - 1) // 2))
                            act.activation(X2H[:, :, P * ((t - 1) % 2):P * ((t - 1) % 2) + P],
                                           M[:, :].rearrange("p (k n) -> p k n", k=KD), ACT.Copy,
                                           scale=XS).then_inc(x2h_ready, 1)
                        if t in (3, 5, 7, 9) and s in (1, 8):
                            k = b * 8 + (t - 3) + (0 if s == 1 else 1)
                            after(act, hp_ready, 4 * k + 4)
                            act.activation(HP[:, :, :], HP[:, :, :], ACT.Gelu).then_inc(gelu_done, 1)

            one_pass(0)
            with act.Fori(1, B) as b:
                one_pass(b)

        @block.vector
        def _(dve):
            setup = [0]

            def link(ins):
                setup[0] += 1
                ins.then_inc(set_chain, 1)
                dve.wait_ge(set_chain, setup[0])

            for j, (w, arrived) in enumerate(((w1f, w1_in), (w2f, w2_in))):
                dve.wait_ge(arrived, 16)
                link(nc.vector.tensor_reduce(wsum[:, j, :], w.rearrange("p (a c) -> p a c", a=64), AX.X, ALU.add,
                                             apply_absolute_value=True))
                nc.vector.tensor_reduce(wtot[:, j:j + 1], wsum[:, j, :], AX.X, ALU.add).then_inc(abs_sum, 1)
            for j, (w, q, arrived) in enumerate(((w1f, W1Q, w1_in), (w2f, W2Q, w2_in))):
                after(dve, abs_all, j + 1)
                link(nc.vector.tensor_scalar(thr[:, j, 0:1], (F, M)[j][:, 0:1], 1.0 / (D * FF), TERNARY_CUT, ALU.mult, ALU.mult))
                link(nc.vector.tensor_scalar(thr[:, j, 1:2], thr[:, j, 0:1], -1.0, None, ALU.mult))
                qf = q[:, :, :].rearrange("p a b -> p (a b)")
                for k in range(4):
                    c = slice(FF * k, FF * (k + 1))
                    link(nc.vector.tensor_scalar(cutt, w[:, c], thr[:, j, 1:2], None, ALU.is_le))
                    ins = nc.vector.scalar_tensor_tensor(out=qf[:, c], in0=w[:, c], scalar=thr[:, j, 0:1], in1=cutt,
                                                         op0=ALU.is_ge, op1=ALU.subtract, saturate=False)
                    link(ins)
                    if k == 3 and j == 1:
                        nc.vector.tensor_copy(wtot[:, 1:2], wtot[:, 0:1]).then_inc(ready, 2)
            dve.wait_ge(w_in, 16 * 15)
            link(nc.vector.tensor_tensor(lamp[:, :, :], lamt[:, 0:4:2, :], lamt[:, 1:4:2, :], ALU.mult))
            nc.vector.tensor_reduce(lams2[:, :], lamp[:, :, :], AX.X, ALU.add).then_inc(lam_prod, 1)
            dve.wait_ge(lam_exp, 1)
            link(nc.vector.tensor_tensor(lams2[:, 0:1], lame[:, 1:2], lame[:, 0:1], ALU.subtract))
            nc.vector.tensor_scalar(neglam[:, :], lams2[:, 0:1], -LAMBDA_INIT, None, ALU.add).then_inc(ready, 1)
            nc.vector.tensor_scalar(WQKV[:, :, 0:D], WQKV[:, :, 0:D], DH ** -0.5, None, ALU.mult).then_inc(ready, 1)
            link(nc.vector.tensor_scalar(subc[:, :], subc[:, :], 1.0 - LAMBDA_INIT, None, ALU.mult))
            nc.vector.tensor_scalar(WO[:, :, :], WO[:, :, :], subc[:, 0:1], None, ALU.mult).then_inc(ready, 1)
            dve.wait_ge(ready, 5)

            def variance(src, nl):
                nc.vector.bn_stats(ST[:, :], src).then_inc(ln_chain, 1)
                hold(dve, ln_chain, 2 * nl + 1)
                nc.vector.bn_aggr(MV[:, :], ST[:, :]).then_inc(ln_chain, 1)
                after(dve, ln_chain, 2 * nl + 2)
                nc.vector.tensor_scalar(VE[:, 0:1], MV[:, 1:2], EPS, None, ALU.add).then_inc(ln_var, 1)

            def normalise(src, nl, done):
                after(dve, ln_rstd, nl + 1)
                nc.vector.tensor_scalar(TOK[:, :], src, MV[:, 0:1], RST[:, 0:1], ALU.subtract, ALU.mult).then_inc(done, 1)

            def rope_mul(nb, tile, part):
                full, c0, n = (m_q, 0, NQ) if part == 0 else (m_kv, D, NK)
                after(dve, full, nb + 1)
                if part == 0:
                    after(dve, m_kt, nb)
                    after(dve, split_done, 2 * nb)
                src = qk3(M[:, 0:n * DH])
                d1, d2 = qk3(T1[:, c0:c0 + n * DH]), qk3(T2[:, c0:c0 + n * DH])
                hd = DH // 2
                cos = ropet[:, 0, tile, :].unsqueeze(1).broadcast_to([P, n, DH])
                sn1 = ropet[:, 1, tile, 0:hd].unsqueeze(1).broadcast_to([P, n, hd])
                sn2 = ropet[:, 1, tile, hd:DH].unsqueeze(1).broadcast_to([P, n, hd])
                nc.vector.tensor_tensor(d1, src, cos, ALU.mult)
                nc.vector.tensor_tensor(d2[:, :, 0:hd], src[:, :, hd:DH], sn1, ALU.mult)
                ins = nc.vector.tensor_tensor(d2[:, :, hd:DH], src[:, :, 0:hd], sn2, ALU.mult)
                if part == 0:
                    ins.then_inc(q_roped, 1)
                else:
                    nc.vector.tensor_copy(V[:, tile, :], M[:, DKV:2 * DKV]).then_inc(kv_roped, 1)

            def rest(nb, part):
                c, n = (slice(0, D), D) if part == 0 else (slice(D, D + DKV), DKV)
                after(dve, high_part, 2 * nb + part + 1)
                nc.vector.tensor_tensor(T2[:, c], M[:, 0:n], SPL[:, 0, c], ALU.subtract).then_inc(rest_part, 1)

            def row_max(b, i, n, k):
                m = (2 * (i * H + n) + k) % 8
                after(dve, s_ready, b * NQ * TILES + i * NQ + 2 * n + k + 1)
                nc.vector.tensor_reduce(NM[:, m:m + 1], score_out(i, 2 * n + k, P * (i + 1)), AX.X, ALU.max,
                                        negate=True).then_inc(max_ready, 1)

            def row_max_pair(b, i, n):
                m = (2 * (i * H + n)) % 8
                k = banks(i, 2 * n)[0]
                after(dve, s_ready, b * NQ * TILES + i * NQ + 2 * n + 2)
                nc.vector.tensor_reduce(NM[:, m:m + 2], SP_[:, k:k + 2, 0:P * (i + 1)], AX.X, ALU.max,
                                        negate=True).then_inc(max_ready, 2)

            def diff(b, i, n):
                u = i * H + n
                gu = b * H * TILES + u
                w = P * (i + 1)
                col = 8 * (n // 8) + 4 * (n % 2) + (n % 8) // 2
                after(dve, exp_done, 2 * gu + 2)
                nc.vector.reciprocal(RS[:, i % 2, :, col], SUM[:, i % 2, :, col]).then_inc(d_chain, 1)
                after(dve, d_chain, 2 * gu + 1)
                nc.vector.tensor_scalar(CC[:, u % 2:u % 2 + 1], SUM[:, i % 2, 0, col:col + 1], RS[:, i % 2, 1, col:col + 1],
                                        neglam[:, 0:1], ALU.mult, ALU.mult).then_inc(d_chain, 1)
                after(dve, d_chain, 2 * gu + 2)
                nc.vector.scalar_tensor_tensor(out=E1[:, u % 2, 0:w], in0=E2[:, 0:w], scalar=CC[:, u % 2:u % 2 + 1],
                                               in1=E1[:, u % 2, 0:w], op0=ALU.mult, op1=ALU.add).then_inc(d_ready, 1)

            dve.wait_ge(x_in[0], 16)
            variance(X[:, 0, :], 0)
            normalise(X[:, 0, :], 0, xn_ready)
            rope_mul(0, 0, 0)
            rope_mul(0, 0, 1)
            rest(0, 0)
            rest(0, 1)
            def one_pass(b):
                for t in range(TILES + 2):
                    nb = built(b, t)
                    tile = next_tile(t)
                    build = tile is not None
                    finish = 1 <= t <= 8
                    nf = b * TILES + t - 1
                    nl = b * (2 * TILES) + 1 + (2 * t - 1 if t else 0)
                    if t == 8:
                        nl = b * (2 * TILES) + 2 * TILES - 1
                    xs = (t + 1) % 4 if t < 8 else 0
                    for s in range(H):
                        if 4 <= t < TILES:
                            row_max(b, t, s, 0)
                        if t < TILES and s >= 1:
                            diff(b, t, s - 1)
                        if 1 <= t <= TILES and s == 0:
                            diff(b, t - 1, H - 1)
                        if 4 <= t < TILES:
                            row_max(b, t, s, 1)
                        if t < 4:
                            row_max_pair(b, t, s)
                        if s == 0 and build:
                            k = b * 4 + (t + 1 if t < 8 else TILES) // 2
                            after(dve, x_in[(t + 1) % 2 if t < 8 else 0], 16 * k + 16)
                            variance(X[:, xs, :], nl)
                        if s == 1 and build:
                            after(dve, m_x2t, b * TILES + (t - 1 if 0 < t else 0))
                            normalise(X[:, xs, :], nl, xn_ready)
                        if s == 3 and build:
                            rope_mul(nb, tile, 0)
                        if s == 4 and build:
                            rope_mul(nb, tile, 1)
                        if s == 5 and finish:
                            after(dve, m_at, nf + 1)
                            nc.vector.tensor_tensor(
                                TOK[:, :].rearrange("p (c d) -> p c d", d=DV), M[:, :].rearrange("p (c d) -> p c d", d=DV),
                                RS[:, (t - 1) % 2, 0, :].unsqueeze(2).broadcast_to([P, H, DV]), ALU.mult).then_inc(attn_ready, 1)
                        if s == 6:
                            if build:
                                rest(nb, 0)
                            if finish:
                                after(dve, sq_ready, nf + 1)
                                nc.vector.tensor_reduce(MS[:, :], SQ[:, :].rearrange("p (c d) -> p c d", d=DV), AX.X,
                                                        ALU.add).then_inc(ms_chain, 1)
                                after(dve, ms_chain, nf + 1)
                                nc.vector.tensor_scalar(VE[:, :], MS[:, :], 1.0 / DV, EPS, ALU.mult, ALU.add).then_inc(ms_ready, 1)
                        if s == 7:
                            if build:
                                rest(nb, 1)
                            if finish:
                                after(dve, rms_ready, nf + 1)
                                tok = TOK[:, :].rearrange("p (c d) -> p c d", d=DV)
                                nc.vector.tensor_tensor(tok, tok, RST[:, :].unsqueeze(2).broadcast_to([P, H, DV]),
                                                        ALU.mult).then_inc(an_ready, 1)
                        if s == 9 and finish:
                            after(dve, m_wo, nf + 1)
                            nc.vector.tensor_tensor(X1[:, (t - 1) % 4, :], M[:, :], X[:, (t - 1) % 4, :],
                                                    ALU.add).then_inc(x1_ready, 1)
                        if s == 10 and finish:
                            after(dve, x1_ready, nf + 1)
                            variance(X1[:, (t - 1) % 4, :], nl + (1 if build else 0))
                        if s == 11 and finish:
                            normalise(X1[:, (t - 1) % 4, :], nl + (1 if build else 0), xn2_ready)
                        if s == 12 and finish:
                            after(dve, x2h_ready, nf + 1)
                            c = slice(P * ((t - 1) % 2), P * ((t - 1) % 2) + P)
                            nc.vector.scalar_tensor_tensor(
                                out=X2L[:, :, c], in0=M[:, :].rearrange("p (k n) -> p k n", k=KD), scalar=XS,
                                in1=X2H[:, :, c], op0=ALU.mult, op1=ALU.subtract).then_inc(x2_ready, 1)
                        k = None
                        if t in (2, 4, 6, 8) and s >= 13:
                            c, k = (t - 2) // 2, s - 13
                        if t in (3, 5, 7, 9) and (s == 0 or 4 <= s <= 7):
                            c, k = (t - 3) // 2, 3 if s == 0 else s
                        if k is not None:
                            nk = b * 32 + 8 * c + k
                            after(dve, f1_ready, nk + 1)
                            if k % 4 == 0:
                                after(dve, h_ready, b * 8 + 2 * c + k // 4)
                            for j in range(2):
                                f = 2 * k + j
                                ins = nc.vector.tensor_scalar(HP[:, f % GELU_F, :], F[:, 2 * P * j:2 * P * (j + 1)], 1.0 / XS,
                                                              b1c[:, f:f + 1], ALU.mult, ALU.add)
                            ins.then_inc(hp_ready, 1)
                        if t in (3, 5, 7, 9) and s in (12, 15):
                            c, j = (t - 3) // 2, 0 if s == 12 else 1
                            k = b * TILES + 2 * c + j
                            after(dve, f2_ready, k + 1)
                            after(dve, o_out, 16 * k)
                            nc.vector.scalar_tensor_tensor(out=OUT[:, :], in0=F[:, :], scalar=1.0 / HS,
                                                           in1=X1[:, (2 * c + j) % 4, :], op0=ALU.mult,
                                                           op1=ALU.add).then_inc(o_sum, 1)

            one_pass(0)
            with dve.Fori(1, B) as b:
                one_pass(b)

        @block.tensor
        def _(pe):
            pe.wait_ge(pool_const, 8)
            for j in range(2):
                after(pe, abs_sum, j + 1)
                pe.matmul((F, M)[j][:, 0:1], onesf[:, :], wtot[:, j:j + 1], start=True, stop=True).then_inc(abs_all, 1)

            def transposes(src, n, done):
                for j in range(n):
                    ins = pe.transpose(M[:, P * j:P * (j + 1)], src[:, P * j:P * (j + 1)], ident[:, :])
                ins.then_inc(done, 1)

            def project(w, c0, done):
                for j in range(KD):
                    ins = pe.matmul(M[:, :], WT[:, P * j:P * (j + 1)], w[:, j, c0:c0 + 512], start=(j == 0), stop=(j == KD - 1))
                ins.then_inc(done, 1)

            def scores(b, i, s):
                j = i * NQ + s
                w = P * (i + 1)
                k = banks(i, s)
                if s == 0:
                    after(pe, stacked, 16 * 2 * PROD * (b * TILES + i + 1))
                after(pe, exp_done, b * NQ * TILES + SLOT_FREE[j])
                q = QST[0:ROWS, i % 2, (s % 8) * 4 + s // 8, :]
                kk = ((s // 2) % 8) * 2 + (s // 2) // 8
                for a in range(0, w, 512):
                    n = min(512, w - a)
                    last = a + n == w
                    pe.matmul(SP_[:, k[a // 512], 0:n], q, KST[0:ROWS, a // P:(a + n) // P, kk, :], start=True, stop=not last)
                ins = pe.matmul(SP_[:, k[(w - P) // 512], (w - P) % 512:(w - P) % 512 + P], identb[:, :], maskb[:, :],
                                start=False, stop=True)
                ins.then_inc(s_ready, 1)

            def diff_transposes(b, i, n, g):
                u = i * H + n
                after(pe, d_ready, b * H * TILES + u + 1)
                after(pe, dt_ready, b * N_T + tg(i, n, g))
                for k in range(4 * g, min(4 * g + 4, i + 1)):
                    ins = pe.transpose(DP[:, P * (k - 4 * g):P * (k - 4 * g + 1)], E1[:, u % 2, P * k:P * (k + 1)], ident[:, :])
                ins.then_inc(t_ready, 1)

            def diff_v(b, i, u, g):
                after(pe, dt_ready, b * N_T + tg(i, HALF * u + HALF - 1, g) + 1)
                if u == 0 and g == 0:
                    after(pe, at_ready, b * TILES + i)
                for k in range(4 * g, min(4 * g + 4, i + 1)):
                    for q in range(4):
                        v = DV * (4 * u + q)
                        ins = pe.matmul(PV[DV * q:DV * (q + 1), 2 * P * u:2 * P * (u + 1)], V[:, k, v:v + DV],
                                        DT[:, k, 2 * q:2 * q + 2, :], start=(k == 0), stop=(k == i), skip_group_check=True)
                ins.then_inc(pv_done, 1)

            pe.wait_ge(xn_ready, 1)
            transposes(TOK, KD, m_xt)
            pe.wait_ge(xt_ready, 1)
            pe.wait_ge(ready, 5)
            project(WQKV, 0, m_q)
            pe.wait_ge(q_roped, 1)
            project(WQKV, D, m_kv)
            pe.wait_ge(kv_roped, 1)
            pe.wait_ge(rope_sum, 1)
            transposes(T1, KD, m_qt)
            pe.wait_ge(rest_part, 1)
            pe.wait_ge(rope_sum, 2)
            transposes(T1[:, D:D + DKV], 2, m_kt)
            pe.wait_ge(ready, 5)
            def one_pass(b):
                for t in range(TILES + 2):
                    nb = built(b, t)
                    build = next_tile(t) is not None
                    finish = 1 <= t <= 8
                    nf = b * TILES + t - 1
                    for s in range(H):
                        i, n = (t, s - LAG) if s >= LAG else (t - 1, s - LAG + H)
                        drain = 0 <= i < TILES
                        pv = None
                        if s == LAG + HALF and t < TILES:
                            pv = (t, 0)
                        if s == LAG and 1 <= t <= TILES:
                            pv = (t - 1, 1)
                        if pv:
                            if t < TILES:
                                scores(b, t, 2 * s)
                            diff_v(b, pv[0], pv[1], 0)
                        if drain:
                            diff_transposes(b, i, n, 0)
                        if t < TILES and not pv:
                            scores(b, t, 2 * s)
                        if pv and groups(pv[0]) == 2:
                            diff_v(b, pv[0], pv[1], 1)
                        if drain and groups(i) == 2:
                            diff_transposes(b, i, n, 1)
                        if t < TILES:
                            scores(b, t, 2 * s + 1)
                        if s == 2 and build:
                            after(pe, xn_ready, nb + 1)
                            after(pe, rest_part, 2 * nb)
                            after(pe, x2_ready, b * TILES + (t - 1 if 0 < t else 0))
                            transposes(TOK, KD, m_xt)
                        if s == 3 and build:
                            after(pe, xt_ready, nb + 1)
                            project(WQKV, 0, m_q)
                        if s == 4 and build:
                            after(pe, q_roped, nb + 1)
                            project(WQKV, D, m_kv)
                        if s == 5 and finish:
                            if build:
                                after(pe, kv_roped, nb + 1)
                            after(pe, at_ready, nf + 1)
                            after(pe, x2_ready, nf)
                            transposes(AT, KD, m_at)
                        if s == 6 and build:
                            if finish:
                                after(pe, attn_ready, nf + 1)
                            after(pe, kv_roped, nb + 1)
                            after(pe, rope_sum, 2 * nb + 1)
                            transposes(T1, KD, m_qt)
                        if s == 7 and build:
                            after(pe, rest_part, 2 * nb + 1)
                            after(pe, rope_sum, 2 * nb + 2)
                            transposes(T1[:, D:D + DKV], 2, m_kt)
                        if s == 8 and finish:
                            if build:
                                after(pe, rest_part, 2 * nb + 2)
                            after(pe, an_ready, nf + 1)
                            transposes(TOK, KD, m_ant)
                        if s == 9 and finish:
                            after(pe, ant_ready, nf + 1)
                            project(WO, 0, m_wo)
                        if s == 12 and finish:
                            after(pe, x1_ready, nf + 1)
                            after(pe, xn2_ready, nf + 1)
                            transposes(TOK, KD, m_x2t)
                        k = None
                        if t in (2, 4, 6, 8) and s >= 13:
                            c, k = (t - 2) // 2, s - 13
                        if t in (3, 5, 7, 9) and (s == 0 or 4 <= s <= 7):
                            c, k = (t - 3) // 2, 3 if s == 0 else s
                        if k is not None:
                            after(pe, x2_ready, b * TILES + 2 * c + 2)
                            after(pe, hp_ready, b * 32 + 8 * c + k)
                            hold(pe, o_sum, b * TILES + 2 * c)
                            for f in (2 * k, 2 * k + 1):
                                for j in range(KD):
                                    for xp in (X2H, X2L):
                                        ins = pe.matmul(F[:, 2 * P * (f % 2):2 * P * (f % 2) + 2 * P],
                                                        W1Q[:, j, P * f:P * (f + 1)], xp[:, j, :],
                                                        start=(j == 0 and xp is X2H), stop=(j == KD - 1 and xp is X2L))
                            ins.then_inc(f1_ready, 1)
                        if t in (3, 5, 7, 9) and s >= 9:
                            c = (t - 3) // 2
                            j = 0 if s <= 12 else 1
                            f0, f1 = {9: (0, 4), 10: (4, 8), 11: (8, 12), 12: (12, 16),
                                      13: (0, 5), 14: (5, 10), 15: (10, 16)}[s]
                            if f0 == 0:
                                after(pe, hp_ready, b * 32 + 8 * c + 8)
                                after(pe, o_sum, b * TILES + 2 * c + j)
                            for f in range(f0, f1):
                                if f in (0, f0, GELU_F):
                                    hold(pe, h_ready, b * 8 + 2 * c + (1 if f < GELU_F else 2))
                                for hp in (HH, HL):
                                    ins = pe.matmul(F[:, :], hp[:, f, P * j:P * (j + 1)], W2Q[:, f, :],
                                                    start=(f == 0 and hp is HH), stop=(f == FT - 1 and hp is HL))
                            if f1 == FT:
                                ins.then_inc(f2_ready, 1)

            one_pass(0)
            with pe.Fori(1, B) as b:
                one_pass(b)


def rope_tables():
    inv = (np.float32(ROPE_THETA) ** (-np.arange(DH, dtype=np.float32) / np.float32(DH))).astype(np.float32)
    f = (np.arange(S, dtype=np.float32)[:, None] * inv[None, :]).astype(np.float32)
    cos, sin = np.cos(f).astype(np.float32), np.sin(f).astype(np.float32)
    sin[:, :DH // 2] *= -1
    t = np.stack([cos, sin])
    return np.ascontiguousarray(t.reshape(2, TILES, P, DH).transpose(2, 0, 1, 3))


def kernel(**inputs):
    import numpy as _np
    import concourse.bacc as _bacc
    from concourse import mybir as _mybir
    from concourse.bass_utils import run_bass_kernel_spmd as _run

    nc = _bacc.Bacc("TRN2", target_bir_lowering=False, num_devices=1)
    a = {k: _np.asarray(v) for k, v in inputs.items()}
    x = a["L0_attn_hidden_states"]
    arrays = {
        "x": _np.concatenate([x, x[:1]], axis=0),
        "wqT": a["L0_attn_Wq"].T, "wkT": a["L0_attn_Wk"].T, "wvT": a["L0_attn_Wv"].T,
        "woT": a["L0_attn_Wo"].T.reshape(2, 4, 2, DV, D).transpose(0, 2, 1, 3, 4).reshape(KD, P, D),
        "lams": _np.stack([a["L0_attn_lambda_q1"], a["L0_attn_lambda_k1"], a["L0_attn_lambda_q2"], a["L0_attn_lambda_k2"]]),
        "subw": a["L0_attn_subln_weight"],
        "w1T": a["L0_ffn_w1"].T, "b1": a["L0_ffn_b1"].reshape(FT, P).T,
        "w2T": a["L0_ffn_w2"].T, "b2": a["L0_ffn_b2"],
        "rope": rope_tables(),
    }
    feeds, args = {}, []
    for name, v in arrays.items():
        v = _np.ascontiguousarray(v)
        feeds[f"in_{name}"] = v
        args.append(nc.dram_tensor(f"in_{name}", v.shape, _mybir.dt.from_np(v.dtype), kind="ExternalInput").ap())
    args.append(nc.dram_tensor("out_0", (B, S, D), F32, kind="ExternalOutput").ap())
    diff_attention_ffn(nc, *args)
    r = _run(nc, [feeds], core_ids=[0])
    return r.results[0]["out_0"]
```

```python
import math
from contextlib import ExitStack

import numpy as np

import concourse.bass as bass
from concourse import mybir

F32 = mybir.dt.float32
F16 = mybir.dt.float16
BF16 = mybir.dt.bfloat16
F8 = mybir.dt.float8e4
ALU = mybir.AluOpType
ACT = mybir.ActivationFunctionType
AX = mybir.AxisListType

P = 128
B, S, D = 8, 1024, 512
H, KVH = 16, 8
DH = D // H // 2
DV = 2 * DH
NQ, NK = 2 * H, 2 * KVH
DKV = NK * DH
FF = 2048
KD = D // P
FT = FF // P
TILES = S // P
HALF = H // 2
EPS = 1e-5
LAMBDA_INIT = 0.8 - 0.6 * math.exp(-0.3 * 2)
ROPE_THETA = 10000.0
TERNARY_CUT = 0.7
MASKED = -1e30
XS = 2048.0
HS = 1.0 / 16
PROD = 6
QPART = (0, 0, 0, 1, 1, 2)
KPART = (0, 1, 2, 0, 1, 0)
ROWS = PROD * DH
GELU_F = FT // 2
HS_TILE = 2 * H



def groups(i):
    return 1 if i < 4 else 2


def tg(i, n, g):
    return (H * i if i < 4 else H * 4 + 2 * H * (i - 4)) + n * groups(i) + g


def pg(i, u, g):
    return (2 * i if i < 4 else 8 + 4 * (i - 4)) + u * groups(i) + g


def banks(i, s):
    return [s % 4] if i < 4 else [2 * (s % 2), 2 * (s % 2) + 1]



def slot_users():
    last = {0: -1, 1: -1, 2: 0, 3: 0}
    need = []
    for i in range(TILES):
        for s in range(NQ):
            need.append(max([last[k] for k in banks(i, s)]))
            for k in banks(i, s):
                last[k] = i * NQ + s + 1
    return need


SLOT_FREE = slot_users()
N_T = tg(TILES - 1, H - 1, 1) + 1
N_PV = pg(TILES - 1, 1, 1) + 1
N_E = NQ * TILES
N_U = H * TILES

LN1_STATS, LN1_ROWS, LN1_TURN = 0, 2, 4
Q_PROJ, Q_ROPE = 5, 7
KV_PROJ, KV_ROPE = 10, 12
Q_TURN, K_TURN = 14, 15
PV_OUT, AT_TURN = 5, 8
MEAN_SQ, RMS_ROWS, AN_TURN = 10, 13, 16
O_PROJ, O_SUM = 17, 19
LN2_STATS, LN2_ROWS, LN2_TURN = 20, 22, 24
W1_EVEN = (25, 27, 29)
W1_ODD = (0, 5, 7, 9, 11)
GELU = (3, 13)
SPLIT_ODD = (3, 4, 5, 6, 13, 14, 15, 16)
W2_ODD, W2_EVEN = 16, 2
V0_MOVE = 5


class QBlock:

    def __init__(self, b, t, kind):
        def runs(start, ends):
            return kind == "loop" or (kind == "first" and t >= start) or (kind == "last" and t in ends)

        even = t % 2 == 0
        self.b, self.t = b, t
        self.attend = kind != "last"
        self.finish = runs(1, (0,))
        self.w1a = even and runs(2, (0,))
        self.w1b = not even and runs(3, (1,))
        self.w2b = even and runs(4, (0, 2))
        self.nb = b * TILES + t + 1
        self.nf = b * TILES + t - 1
        self.pair = b * (TILES // 2) + t // 2 - 1
        self.no = b * TILES + t - 3
        self.next = (t + 1) % TILES

    def before(self, n):
        if n >= 0:
            return (self.b, self.t, n) if self.attend else None
        if not self.finish:
            return None
        return (self.b, self.t - 1, n + H) if self.t else (self.b - 1, TILES - 1, n + H)

    def first_piece(self, h):
        at = W1_EVEN if self.w1a else W1_ODD if self.w1b else ()
        for n, h0 in enumerate(at):
            if h in (h0, h0 + 1):
                return (n if self.w1a else n + 3), h - h0
        return None


def every_block(eng, run):
    for t in range(TILES):
        run(QBlock(0, t, "first"))
    with eng.Fori(1, B) as b:
        for t in range(TILES):
            run(QBlock(b, t, "loop"))
    for t in range(3):
        run(QBlock(B, t, "last"))


def diff_attention_ffn(nc, x, wqT, wkT, wvT, woT, lams, subw, w1T, b1, w2T, b2, rope, out):
    ctx = ExitStack()
    with ctx:
        def sb(name, shape, dt):
            return ctx.enter_context(nc.sbuf_tensor(name, shape, dt))

        def sem(name):
            return ctx.enter_context(nc.semaphore(name))

        WQKV = sb("WQKV", [P, KD, D + 2 * DKV], F32)
        WO = sb("WO", [P, KD, D], F32)
        W1Q = sb("W1Q", [P, KD, FF], F8)
        W2Q = sb("W2Q", [P, FT, D], F8)
        ident = sb("ident", [P, P], F32)
        identb = sb("identb", [P, P], BF16)
        maskb = sb("maskb", [P, P], BF16)
        nhalf = sb("nhalf", [P, H], F32)
        ropet = sb("ropet", [P, 2, TILES, DH], F32)
        b1c = sb("b1c", [P, FT], F32)
        b2b = sb("b2b", [P, D], F32)
        subc = sb("subc", [P, 1], F32)
        lamt = sb("lamt", [P, 4, DH], F32)
        lamp = sb("lamp", [P, 2, DH], F32)
        lams2 = sb("lams2", [P, 2], F32)
        lame = sb("lame", [P, 2], F32)
        neglam = sb("neglam", [P, 1], F32)
        wtot = sb("wtot", [P, 2], F32)
        thr = sb("thr", [P, 2, 2], F32)
        KST = sb("KST", [P, TILES, NK, P], BF16)
        QST = sb("QST", [P, 2, NQ, P], BF16)
        V = sb("V", [P, TILES, DKV], F32)
        E1 = sb("E1", [P, 2, S], F32)
        E2 = sb("E2", [P, S], F32)
        DT = sb("DT", [P, TILES, HALF, P], F32)
        NM = sb("NM", [P, 8], F32)
        SUM = sb("SUM", [P, 2, 2, H], F32)
        RS = sb("RS", [P, 2, 2, H], F32)
        CC = sb("CC", [P, 2], F32)
        VST = sb("VST", [P, DKV], F32)
        X = sb("X", [P, 4, D], F32)
        TOK = sb("TOK", [P, D], F32)
        WT = sb("WT", [P, D], F32)
        ST = sb("ST", [P, 6], F32)
        MV = sb("MV", [P, 2], F32)
        VE = sb("VE", [P, H], F32)
        RST = sb("RST", [P, H], F32)
        T1 = sb("T1", [P, D + DKV], F32)
        T2 = sb("T2", [P, D + DKV], F32)
        SPL = sb("SPL", [P, 3, D + DKV], BF16)
        AT = sb("AT", [P, D], F32)
        SQ = AT
        MS = sb("MS", [P, H], F32)
        X1 = sb("X1", [P, 4, D], F32)
        X2H = sb("X2H", [P, KD, 2 * P], F16)
        X2L = sb("X2L", [P, KD, 2 * P], F16)
        HP = sb("HP", [P, GELU_F, 2 * P], F32)
        HH = sb("HH", [P, FT, 2 * P], F16)
        HL = sb("HL", [P, FT, 2 * P], F16)
        OUT = AT

        SP_ = ctx.enter_context(nc.psum_tensor("SP_", [P, 4, 512], F32))
        DP = ctx.enter_context(nc.psum_tensor("DP", [P, 512], F32))
        PV = ctx.enter_context(nc.psum_tensor("PV", [P, 512], F32))
        M = ctx.enter_context(nc.psum_tensor("M", [P, 512], F32))
        F = ctx.enter_context(nc.psum_tensor("F", [P, 512], F32))

        scratch = nc.dram_tensor("scratch", [2, P, 3, D + DKV], BF16, kind="Internal").ap()

        w_in = sem("w_in")
        w1_in = sem("w1_in")
        w2_in = sem("w2_in")
        pool_const = sem("pool_const")
        lam_prod = sem("lam_prod")
        lam_exp = sem("lam_exp")
        set_chain = sem("set_chain")
        abs_sum = sem("abs_sum")
        abs_all = sem("abs_all")
        ready = sem("ready")
        x_in = [sem("x_in_even"), sem("x_in_odd")]
        ln_chain = [sem("ln1_chain"), sem("ln2_chain")]
        ln_var = [sem("ln1_var"), sem("ln2_var")]
        ln_rstd = [sem("ln1_rstd"), sem("ln2_rstd")]
        xn_ready = sem("xn_ready")
        m_xt = sem("m_xt")
        xt_ready = sem("xt_ready")
        m_q = sem("m_q")
        q_roped = sem("q_roped")
        m_kv = sem("m_kv")
        kv_roped = sem("kv_roped")
        v0_moved = sem("v0_moved")
        rope_sum = sem("rope_sum")
        m_qt = sem("m_qt")
        m_kt = sem("m_kt")
        high_part = sem("high_part")
        rest_part = sem("rest_part")
        mid_part = sem("mid_part")
        split_done = sem("split_done")
        scr_out = sem("scr_out")
        stacked = sem("stacked")
        s_ready = sem("s_ready")
        max_ready = sem("max_ready")
        exp_done = sem("exp_done")
        d_chain = sem("d_chain")
        d_ready = sem("d_ready")
        t_ready = sem("t_ready")
        dt_ready = sem("dt_ready")
        pv_done = sem("pv_done")
        at_ready = sem("at_ready")
        m_at = sem("m_at")
        attn_ready = sem("attn_ready")
        sq_ready = sem("sq_ready")
        ms_chain = sem("ms_chain")
        ms_ready = sem("ms_ready")
        rms_ready = sem("rms_ready")
        an_ready = sem("an_ready")
        m_ant = sem("m_ant")
        ant_ready = sem("ant_ready")
        m_wo = sem("m_wo")
        x1_ready = sem("x1_ready")
        xn2_ready = sem("xn2_ready")
        m_x2t = sem("m_x2t")
        x2h_ready = sem("x2h_ready")
        x2_ready = sem("x2_ready")
        f1_ready = sem("f1_ready")
        hp_ready = sem("hp_ready")
        gelu_done = sem("gelu_done")
        h_chain = sem("h_chain")
        h_ready = sem("h_ready")
        f2_ready = sem("f2_ready")
        o_sum = sem("o_sum")
        o_ready = sem("o_ready")
        o_out = sem("o_out")
        held = sem("held")

        onesf = E1[:, 0, 0:P]
        wsum = E1[:, 1, 0:2 * 64].rearrange("p (a b) -> p a b", b=64)
        w1f = DT[:, :, :, :].rearrange("p a b c -> p (a b c)")
        w2f = KST[:, :, :, :].rearrange("p a b c -> p (a b c)").bitcast(F32)
        cutt = HP[:, :, :].rearrange("p a b -> p (a b)")

        def hold(eng, signal, value):
            if not isinstance(value, int) or value > 0:
                eng.wait_ge(signal, value)
                eng.sem_inc(held, 1)

        def after(eng, signal, value):
            if not isinstance(value, int) or value > 0:
                eng.wait_ge(signal, value)

        def score_out(i, s, w):
            k = banks(i, s)
            return SP_[:, k[0]:k[0] + len(k), :].rearrange("p a b -> p (a b)")[:, 0:w]

        def qk3(ap):
            return ap.rearrange("p (s d) -> p s d", d=DH)

        block = ctx.enter_context(nc.Block())

        @block.sync
        def _(sp):
            sp.dma_start(w1f.rearrange("p (k n) -> p k n", k=KD), w1T.rearrange("(k p) n -> p k n", p=P)).then_inc(w1_in, 16)
            sp.dma_start(w2f.rearrange("p (k n) -> p k n", k=FT), w2T.rearrange("(k p) n -> p k n", p=P)).then_inc(w2_in, 16)
            for j in range(2):
                sp.dma_start(X[:, j, :], x[0, j * P:(j + 1) * P, :]).then_inc(x_in[j], 16)
            sp.dma_start(WQKV[:, :, 0:D], wqT.rearrange("(k p) n -> p k n", p=P)).then_inc(w_in, 16)
            sp.dma_start(WQKV[:, :, D:D + DKV], wkT.rearrange("(k p) n -> p k n", p=P)).then_inc(w_in, 16)
            sp.dma_start(WQKV[:, :, D + DKV:D + 2 * DKV], wvT.rearrange("(k p) n -> p k n", p=P)).then_inc(w_in, 16)
            sp.dma_start(WO[:, :, :], woT.rearrange("k p n -> p k n")).then_inc(w_in, 16)
            sp.dma_start(ropet[:, :, :, :], rope).then_inc(w_in, 16)
            sp.dma_start(b1c[:, :], b1).then_inc(w_in, 16)
            sp.dma_start(b2b[:, :], b2.partition_broadcast(P)).then_inc(w_in, 16)
            for j in range(4):
                sp.dma_start(lamt[:, j, :], lams[j].partition_broadcast(P)).then_inc(w_in, 16)
                sp.dma_start(subc[DV * j:DV * (j + 1), :], subw.unsqueeze(1)).then_inc(w_in, 16)

            def stack(nb, tile, q_free, k_free):
                hold(sp, stacked, 16 * 2 * PROD * (nb - 1))
                hold(sp, split_done, 2 * nb + 2)
                sp.dma_start(scratch[tile % 2], SPL[:, :, :]).then_inc(scr_out, 16)
                hold(sp, scr_out, 16 * nb + 16)
                src = scratch[tile % 2].rearrange("(s d) a (c n) -> a d s c n", d=DH, n=P)
                hold(sp, s_ready, q_free)
                for j in range(PROD):
                    sp.dma_start(QST[DH * j:DH * (j + 1), tile % 2, :, :].rearrange("p (s c) n -> p s c n", s=8),
                                 src[QPART[j], :, :, 0:4, :]).then_inc(stacked, 16)
                if k_free is not None:
                    hold(sp, s_ready, k_free)
                for j in range(PROD):
                    sp.dma_start(KST[DH * j:DH * (j + 1), tile, :, :].rearrange("p (s c) n -> p s c n", s=8),
                                 src[KPART[j], :, :, 4:6, :]).then_inc(stacked, 16)

            def dma_work(T):
                b, t = T.b, T.t
                if T.attend:
                    j = (t + 2) % TILES
                    hold(sp, x1_ready, T.nf)
                    row = x[b] if t < TILES - 2 else x[b + 1]
                    sp.dma_start(X[:, j % 4, :], row[j * P:(j + 1) * P, :]).then_inc(x_in[t % 2], 16)
                    stack(T.nb, T.next, b * N_E + t * NQ, (b + 1) * N_E if t == TILES - 1 else None)
                if T.w1b or T.w2b:
                    hold(sp, o_ready, T.no + 1)
                    rows = out[b, (t - 3) * P:(t - 2) * P, :] if t >= 3 else out[b - 1, (t + 5) * P:(t + 6) * P, :]
                    sp.dma_start(rows, OUT[:, :]).then_inc(o_out, 16)

            sp.wait_ge(ready, 5)
            stack(0, 0, 0, None)
            every_block(sp, dma_work)
            sp.wait_ge(o_out, 16 * B * TILES)
            sp.wait_ge(x_in[0], 16 * (B * TILES // 2 + 1))
            sp.wait_ge(x_in[1], 16 * (B * TILES // 2 + 1))
            sp.wait_ge(stacked, 16 * 2 * PROD * (B * TILES + 1))

        @block.gpsimd
        def _(pool):
            pool.memset(ident[:, :], 0.0).then_inc(pool_const, 1)
            pool.memset(identb[:, :], 0.0).then_inc(pool_const, 1)
            pool.memset(maskb[:, :], 0.0).then_inc(pool_const, 1)
            pool.memset(onesf, 1.0).then_inc(pool_const, 1)
            pool.memset(nhalf[:, :], -0.5).then_inc(pool_const, 1)
            pool.wait_ge(pool_const, 5)
            for m in (ident, identb):
                pool.affine_select(out=m[:, :], in_=m[:, :], compare_op=ALU.not_equal, fill=1.0,
                                   base=0, pattern=[[-1, P]], channel_multiplier=1).then_inc(pool_const, 1)
            pool.affine_select(out=maskb[:, :], in_=maskb[:, :], compare_op=ALU.is_ge, fill=MASKED,
                               base=0, pattern=[[-1, P]], channel_multiplier=1).then_inc(pool_const, 1)
            pool.wait_ge(pool_const, 8)

            def rstd(j, n):
                after(pool, ln_var[j], n + 1)
                pool.tensor_tensor(RST[:, 0:1], VE[:, 0:1], nhalf[:, 0:1], ALU.pow).then_inc(ln_rstd[j], 1)

            def rope_add(nb, part):
                c = slice(0, D) if part == 0 else slice(D, D + DKV)
                after(pool, q_roped if part == 0 else kv_roped, nb + 1)
                pool.tensor_tensor(T1[:, c], T1[:, c], T2[:, c], ALU.add).then_inc(rope_sum, 1)

            def split(nb, part):
                c = slice(0, D) if part == 0 else slice(D, D + DKV)
                hold(pool, rest_part, 2 * nb + part + 1)
                pool.tensor_scalar(SPL[:, 1, c], T2[:, c], 1.0, 0.0, ALU.mult, ALU.add).then_inc(mid_part, 1)
                after(pool, mid_part, 2 * nb + part + 1)
                pool.tensor_tensor(SPL[:, 2, c], T2[:, c], SPL[:, 1, c], ALU.subtract).then_inc(split_done, 1)

            def hidden_split(q, k):
                n = 8 * q + k
                h = slice(2 * k % GELU_F, 2 * k % GELU_F + 2)
                fs = slice(2 * k, 2 * k + 2)
                after(pool, gelu_done, 2 * q + k // 4 + 1)
                hold(pool, f2_ready, 2 * q)
                pool.tensor_scalar(HH[:, fs, :], HP[:, h, :], HS, 0.0, ALU.mult, ALU.add).then_inc(h_chain, 1)
                hold(pool, h_chain, 2 * n + 1)
                pool.tensor_scalar(HP[:, h, :], HP[:, h, :], HS, 0.0, ALU.mult, ALU.add).then_inc(h_chain, 1)
                after(pool, h_chain, 2 * n + 2)
                pool.tensor_tensor(HL[:, fs, :], HP[:, h, :], HH[:, fs, :], ALU.subtract).then_inc(h_ready, 1)

            def pool_work(T):
                for hs in range(HS_TILE):
                    if T.attend:
                        if hs == LN1_STATS:
                            rstd(0, T.nb)
                        if hs == V0_MOVE and T.t == 0:
                            hold(pool, pv_done, T.b * N_PV)
                            hold(pool, kv_roped, T.nb)
                            pool.tensor_copy(V[:, 0, :], VST[:, :]).then_inc(v0_moved, 1)
                        if hs == Q_ROPE:
                            rope_add(T.nb, 0)
                        if hs == KV_ROPE:
                            rope_add(T.nb, 1)
                    if T.finish:
                        if hs == AT_TURN:
                            after(pool, attn_ready, T.nf + 1)
                            pool.tensor_tensor(SQ[:, :], TOK[:, :], TOK[:, :], ALU.mult).then_inc(sq_ready, 1)
                        if hs == MEAN_SQ:
                            after(pool, ms_ready, T.nf + 1)
                            pool.tensor_tensor(RST[:, :], VE[:, :], nhalf[:, :], ALU.pow).then_inc(rms_ready, 1)
                        if hs == LN2_STATS:
                            rstd(1, T.nf)
                    if T.attend and hs == Q_TURN:
                        split(T.nb, 0)
                    if T.attend and hs == K_TURN:
                        split(T.nb, 1)
                    if T.w1b and hs in SPLIT_ODD:
                        hidden_split(T.pair, SPLIT_ODD.index(hs))
                    if (T.w1b and hs == W2_ODD + FT - 1) or (T.w2b and hs == W2_EVEN + FT - 1):
                        after(pool, o_sum, T.no + 1)
                        pool.tensor_tensor(OUT[:, :], OUT[:, :], b2b[:, :], ALU.add).then_inc(o_ready, 1)

            rstd(0, 0)
            rope_add(0, 0)
            rope_add(0, 1)
            split(0, 0)
            split(0, 1)
            every_block(pool, pool_work)

        @block.scalar
        def _(act):
            act.wait_ge(lam_prod, 1)
            act.activation(lame[:, :], lams2[:, :], ACT.Exp).then_inc(lam_exp, 1)

            def xt_copy(nb, wo_done):
                after(act, m_xt, nb + 1)
                after(act, m_wo, wo_done)
                act.activation(WT[:, :], M[:, :], ACT.Copy).then_inc(xt_ready, 1)

            def high(nb, part):
                c, n = (slice(0, D), D) if part == 0 else (slice(D, D + DKV), DKV)
                after(act, m_qt if part == 0 else m_kt, nb + 1)
                if part == 0:
                    after(act, scr_out, 16 * nb)
                act.activation(SPL[:, 0, c], M[:, 0:n], ACT.Copy).then_inc(high_part, 1)

            def exp(T, n, k):
                b, i = T.b, T.t
                u = i * H + n
                w = P * (i + 1)
                after(act, max_ready, b * N_E + 2 * u + k + 1)
                if k == 0:
                    old = T.before(n - 2)
                    if old:
                        pb, pi, pn = old
                        after(act, t_ready, pb * N_T + tg(pi, pn, groups(pi) - 1) + 1)
                    dst = E1[:, u % 2, 0:w]
                else:
                    after(act, d_ready, b * N_U + u - (1 if i < 4 and u > 0 else 0))
                    e = 512 * (u % 2) if i < 4 else 0
                    dst = E2[:, e:e + w]
                col = 8 * (n // 8) + 4 * (n % 2) + (n % 8) // 2
                act.activation(dst, score_out(i, 2 * n + k, w), ACT.Exp, bias=NM[:, (2 * u + k) % 8:(2 * u + k) % 8 + 1],
                               scale=1.0, accum_out=SUM[:, i % 2, k, col:col + 1]).then_inc(exp_done, 1)

            def dt_copy(b, i, n, g):
                k0, k1 = 4 * g, min(4 * g + 4, i + 1)
                after(act, t_ready, b * N_T + tg(i, n, g) + 1)
                if n % HALF == 0:
                    if n or i:
                        pi, pu = (i, 0) if n else (i - 1, 1)
                        after(act, pv_done, b * N_PV + pg(pi, pu, min(g, groups(pi) - 1)) + 1)
                    else:
                        after(act, pv_done, b * N_PV - 1)
                act.activation(DT[:, k0:k1, n % HALF, :], DP[:, 0:P * (k1 - k0)].rearrange("p (k q) -> p k q", q=P),
                               ACT.Copy).then_inc(dt_ready, 1)

            def act_work(T):
                t, nb, nf = T.t, T.nb, T.nf
                for hs in range(HS_TILE):
                    s, h = divmod(hs, 2)
                    old = T.before(s - 1) if h else T.before(s - 2)
                    if old and (h == 1 or groups(old[1]) == 2):
                        dt_copy(*old, 1 - h)
                    if T.attend:
                        exp(T, s, h)
                    if T.attend and hs == LN1_TURN:
                        xt_copy(nb, nf)
                    if T.finish and hs == PV_OUT:
                        pb, pi, _ = T.before(-1)
                        after(act, pv_done, pb * N_PV + pg(pi, 1, groups(pi) - 1) + 1)
                        after(act, ms_ready, nf)
                        after(act, o_out, 16 * T.no)
                        act.activation(AT[:, :], PV[:, :], ACT.Copy).then_inc(at_ready, 1)
                    if T.attend and hs == Q_TURN:
                        high(nb, 0)
                    if T.attend and hs == K_TURN:
                        high(nb, 1)
                    if T.finish and hs == AN_TURN:
                        after(act, m_ant, nf + 1)
                        if T.attend:
                            after(act, m_kv, nb + 1)
                        act.activation(WT[:, :], M[:, :], ACT.Copy).then_inc(ant_ready, 1)
                    if T.finish and hs == LN2_TURN:
                        after(act, m_x2t, nf + 1)
                        if t % 2:
                            after(act, f1_ready, 8 * (T.pair + 1))
                        act.activation(X2H[:, :, P * ((t - 1) % 2):P * ((t - 1) % 2) + P],
                                       M[:, :].rearrange("p (k n) -> p k n", k=KD), ACT.Copy, scale=XS).then_inc(x2h_ready, 1)
                    piece = T.first_piece(hs)
                    if piece and piece[1] == 1:
                        k, n = piece[0], 8 * T.pair + piece[0]
                        after(act, f1_ready, n + 1)
                        after(act, h_ready, n - 3)
                        for f in (2 * k, 2 * k + 1):
                            ins = act.activation(HP[:, f % GELU_F, :], F[:, 2 * P * (f % 2):2 * P * (f % 2) + 2 * P],
                                                 ACT.Identity, bias=b1c[:, f:f + 1], scale=1.0 / XS)
                        ins.then_inc(hp_ready, 1)
                    if T.w1b and hs in GELU:
                        j = GELU.index(hs)
                        after(act, hp_ready, 8 * T.pair + 4 * j + 4)
                        act.activation(HP[:, :, :], HP[:, :, :], ACT.Gelu).then_inc(gelu_done, 1)

            xt_copy(0, 0)
            high(0, 0)
            high(0, 1)
            every_block(act, act_work)

        @block.vector
        def _(dve):
            setup = [0]

            def link(ins):
                setup[0] += 1
                ins.then_inc(set_chain, 1)
                dve.wait_ge(set_chain, setup[0])

            for j, (w, arrived) in enumerate(((w1f, w1_in), (w2f, w2_in))):
                dve.wait_ge(arrived, 16)
                link(nc.vector.tensor_reduce(wsum[:, j, :], w.rearrange("p (a c) -> p a c", a=64), AX.X, ALU.add,
                                             apply_absolute_value=True))
                nc.vector.tensor_reduce(wtot[:, j:j + 1], wsum[:, j, :], AX.X, ALU.add).then_inc(abs_sum, 1)
            for j, (w, q, arrived) in enumerate(((w1f, W1Q, w1_in), (w2f, W2Q, w2_in))):
                after(dve, abs_all, j + 1)
                link(nc.vector.tensor_scalar(thr[:, j, 0:1], (F, M)[j][:, 0:1], 1.0 / (D * FF), TERNARY_CUT, ALU.mult, ALU.mult))
                link(nc.vector.tensor_scalar(thr[:, j, 1:2], thr[:, j, 0:1], -1.0, None, ALU.mult))
                qf = q[:, :, :].rearrange("p a b -> p (a b)")
                for k in range(4):
                    c = slice(FF * k, FF * (k + 1))
                    link(nc.vector.tensor_scalar(cutt, w[:, c], thr[:, j, 1:2], None, ALU.is_le))
                    ins = nc.vector.scalar_tensor_tensor(out=qf[:, c], in0=w[:, c], scalar=thr[:, j, 0:1], in1=cutt,
                                                         op0=ALU.is_ge, op1=ALU.subtract, saturate=False)
                    link(ins)
                    if k == 3 and j == 1:
                        nc.vector.tensor_copy(wtot[:, 1:2], wtot[:, 0:1]).then_inc(ready, 2)
            dve.wait_ge(w_in, 16 * 15)
            link(nc.vector.tensor_tensor(lamp[:, :, :], lamt[:, 0:4:2, :], lamt[:, 1:4:2, :], ALU.mult))
            nc.vector.tensor_reduce(lams2[:, :], lamp[:, :, :], AX.X, ALU.add).then_inc(lam_prod, 1)
            dve.wait_ge(lam_exp, 1)
            link(nc.vector.tensor_tensor(lams2[:, 0:1], lame[:, 1:2], lame[:, 0:1], ALU.subtract))
            nc.vector.tensor_scalar(neglam[:, :], lams2[:, 0:1], -LAMBDA_INIT, None, ALU.add).then_inc(ready, 1)
            nc.vector.tensor_scalar(WQKV[:, :, 0:D], WQKV[:, :, 0:D], DH ** -0.5, None, ALU.mult).then_inc(ready, 1)
            link(nc.vector.tensor_scalar(subc[:, :], subc[:, :], 1.0 - LAMBDA_INIT, None, ALU.mult))
            nc.vector.tensor_scalar(WO[:, :, :], WO[:, :, :], subc[:, 0:1], None, ALU.mult).then_inc(ready, 1)
            dve.wait_ge(ready, 5)

            def variance(j, src, n):
                nc.vector.bn_stats(ST[:, :], src).then_inc(ln_chain[j], 1)
                hold(dve, ln_chain[j], 2 * n + 1)
                nc.vector.bn_aggr(MV[:, :], ST[:, :]).then_inc(ln_chain[j], 1)
                after(dve, ln_chain[j], 2 * n + 2)
                nc.vector.tensor_scalar(VE[:, 0:1], MV[:, 1:2], EPS, None, ALU.add).then_inc(ln_var[j], 1)

            def normalise(j, src, n, done):
                after(dve, ln_rstd[j], n + 1)
                nc.vector.tensor_scalar(TOK[:, :], src, MV[:, 0:1], RST[:, 0:1], ALU.subtract, ALU.mult).then_inc(done, 1)

            def rope_mul(nb, tile, part, moved=0):
                full, c0, n = (m_q, 0, NQ) if part == 0 else (m_kv, D, NK)
                after(dve, full, nb + 1)
                if part == 0:
                    after(dve, m_kt, nb)
                    after(dve, split_done, 2 * nb)
                src = qk3(M[:, 0:n * DH])
                d1, d2 = qk3(T1[:, c0:c0 + n * DH]), qk3(T2[:, c0:c0 + n * DH])
                hd = DH // 2
                cos = ropet[:, 0, tile, :].unsqueeze(1).broadcast_to([P, n, DH])
                sn1 = ropet[:, 1, tile, 0:hd].unsqueeze(1).broadcast_to([P, n, hd])
                sn2 = ropet[:, 1, tile, hd:DH].unsqueeze(1).broadcast_to([P, n, hd])
                nc.vector.tensor_tensor(d1, src, cos, ALU.mult)
                nc.vector.tensor_tensor(d2[:, :, 0:hd], src[:, :, hd:DH], sn1, ALU.mult)
                ins = nc.vector.tensor_tensor(d2[:, :, hd:DH], src[:, :, 0:hd], sn2, ALU.mult)
                if part == 0:
                    ins.then_inc(q_roped, 1)
                else:
                    if tile == 0:
                        after(dve, v0_moved, moved)
                    v = V[:, tile, :] if tile else VST[:, :]
                    nc.vector.tensor_copy(v, M[:, DKV:2 * DKV]).then_inc(kv_roped, 1)

            def rest(nb, part):
                c, n = (slice(0, D), D) if part == 0 else (slice(D, D + DKV), DKV)
                after(dve, high_part, 2 * nb + part + 1)
                nc.vector.tensor_tensor(T2[:, c], M[:, 0:n], SPL[:, 0, c], ALU.subtract).then_inc(rest_part, 1)

            def row_max(b, i, n, k):
                m = (2 * (i * H + n) + k) % 8
                after(dve, s_ready, b * N_E + i * NQ + 2 * n + k + 1)
                nc.vector.tensor_reduce(NM[:, m:m + 1], score_out(i, 2 * n + k, P * (i + 1)), AX.X, ALU.max,
                                        negate=True).then_inc(max_ready, 1)

            def row_max_pair(b, i, n):
                m = (2 * (i * H + n)) % 8
                k = banks(i, 2 * n)[0]
                after(dve, s_ready, b * N_E + i * NQ + 2 * n + 2)
                nc.vector.tensor_reduce(NM[:, m:m + 2], SP_[:, k:k + 2, 0:P * (i + 1)], AX.X, ALU.max,
                                        negate=True).then_inc(max_ready, 2)

            def diff(b, i, n):
                u = i * H + n
                gu = b * N_U + u
                w = P * (i + 1)
                e = 512 * (u % 2) if i < 4 else 0
                col = 8 * (n // 8) + 4 * (n % 2) + (n % 8) // 2
                after(dve, exp_done, 2 * gu + 2)
                nc.vector.reciprocal(RS[:, i % 2, :, col], SUM[:, i % 2, :, col]).then_inc(d_chain, 1)
                after(dve, d_chain, 2 * gu + 1)
                nc.vector.scalar_tensor_tensor(out=CC[:, u % 2:u % 2 + 1], in0=SUM[:, i % 2, 0, col:col + 1], scalar=neglam[:, 0:1],
                                               in1=RS[:, i % 2, 1, col:col + 1], op0=ALU.mult, op1=ALU.mult).then_inc(d_chain, 1)
                after(dve, d_chain, 2 * gu + 2)
                nc.vector.scalar_tensor_tensor(out=E1[:, u % 2, 0:w], in0=E2[:, e:e + w], scalar=CC[:, u % 2:u % 2 + 1],
                                               in1=E1[:, u % 2, 0:w], op0=ALU.mult, op1=ALU.add).then_inc(d_ready, 1)

            def dve_work(T):
                b, t, nb, nf = T.b, T.t, T.nb, T.nf
                for hs in range(HS_TILE):
                    s, h = divmod(hs, 2)
                    if T.attend:
                        if t >= 4:
                            row_max(b, t, s, h)
                        elif h == 0:
                            row_max_pair(b, t, s)
                    if h == 0 and T.before(s - 1):
                        diff(*T.before(s - 1))
                    if T.attend:
                        slot = X[:, (t + 1) % 4, :]
                        if hs == LN1_STATS:
                            after(dve, x_in[(t + 1) % 2], 16 * (b * (TILES // 2) + (t + 1) // 2) + 16)
                            variance(0, slot, nb)
                        if hs == LN1_ROWS:
                            after(dve, m_x2t, nf)
                            normalise(0, slot, nb, xn_ready)
                        if hs == Q_ROPE:
                            rope_mul(nb, T.next, 0)
                        if hs == KV_ROPE:
                            rope_mul(nb, T.next, 1, b + 1)
                        if hs == Q_TURN:
                            rest(nb, 0)
                        if hs == K_TURN:
                            rest(nb, 1)
                    if T.finish:
                        tok = TOK[:, :].rearrange("p (c d) -> p c d", d=DV)
                        x1 = X1[:, (t - 1) % 4, :]
                        if hs == AT_TURN:
                            after(dve, m_at, nf + 1)
                            if T.attend:
                                after(dve, m_xt, nb + 1)
                            nc.vector.tensor_tensor(tok, M[:, :].rearrange("p (c d) -> p c d", d=DV),
                                                    RS[:, (t - 1) % 2, 0, :].unsqueeze(2).broadcast_to([P, H, DV]),
                                                    ALU.mult).then_inc(attn_ready, 1)
                        if hs == MEAN_SQ:
                            after(dve, sq_ready, nf + 1)
                            nc.vector.tensor_reduce(MS[:, :], SQ[:, :].rearrange("p (c d) -> p c d", d=DV), AX.X,
                                                    ALU.add).then_inc(ms_chain, 1)
                            after(dve, ms_chain, nf + 1)
                            nc.vector.tensor_scalar(VE[:, :], MS[:, :], 1.0 / DV, EPS, ALU.mult, ALU.add).then_inc(ms_ready, 1)
                        if hs == RMS_ROWS:
                            after(dve, rms_ready, nf + 1)
                            nc.vector.tensor_tensor(tok, tok, RST[:, :].unsqueeze(2).broadcast_to([P, H, DV]),
                                                    ALU.mult).then_inc(an_ready, 1)
                        if hs == O_SUM:
                            after(dve, m_wo, nf + 1)
                            nc.vector.tensor_tensor(x1, M[:, :], X[:, (t - 1) % 4, :], ALU.add).then_inc(x1_ready, 1)
                        if hs == LN2_STATS:
                            after(dve, x1_ready, nf + 1)
                            variance(1, x1, nf)
                        if hs == LN2_ROWS:
                            after(dve, m_ant, nf + 1)
                            normalise(1, x1, nf, xn2_ready)
                        if hs == LN2_TURN:
                            after(dve, x2h_ready, nf + 1)
                            c = slice(P * ((t - 1) % 2), P * ((t - 1) % 2) + P)
                            nc.vector.scalar_tensor_tensor(
                                out=X2L[:, :, c], in0=M[:, :].rearrange("p (k n) -> p k n", k=KD), scalar=XS,
                                in1=X2H[:, :, c], op0=ALU.mult, op1=ALU.subtract).then_inc(x2_ready, 1)
                    if (T.w1b and hs == W2_ODD + FT - 1) or (T.w2b and hs == W2_EVEN + FT - 1):
                        after(dve, f2_ready, T.no + 1)
                        after(dve, o_out, 16 * T.no)
                        nc.vector.scalar_tensor_tensor(out=OUT[:, :], in0=F[:, :], scalar=1.0 / HS,
                                                       in1=X1[:, (t - 3) % 4, :], op0=ALU.mult,
                                                       op1=ALU.add).then_inc(o_sum, 1)

            dve.wait_ge(x_in[0], 16)
            variance(0, X[:, 0, :], 0)
            normalise(0, X[:, 0, :], 0, xn_ready)
            rope_mul(0, 0, 0)
            rope_mul(0, 0, 1)
            rest(0, 0)
            rest(0, 1)
            every_block(dve, dve_work)

        @block.tensor
        def _(pe):
            pe.wait_ge(pool_const, 8)
            for j in range(2):
                after(pe, abs_sum, j + 1)
                pe.matmul((F, M)[j][:, 0:1], onesf, wtot[:, j:j + 1], start=True, stop=True).then_inc(abs_all, 1)

            def transposes(src, n, done):
                for j in range(n):
                    ins = pe.transpose(M[:, P * j:P * (j + 1)], src[:, P * j:P * (j + 1)], ident[:, :])
                ins.then_inc(done, 1)

            def project(w, c0, js, done):
                for j in js:
                    ins = pe.matmul(M[:, :], WT[:, P * j:P * (j + 1)], w[:, j, c0:c0 + 512], start=(j == 0), stop=(j == KD - 1))
                if js[-1] == KD - 1:
                    ins.then_inc(done, 1)

            def scores(b, i, s):
                w = P * (i + 1)
                k = banks(i, s)
                if s == 0:
                    after(pe, stacked, 16 * 2 * PROD * (b * TILES + i + 1))
                after(pe, exp_done, b * N_E + SLOT_FREE[i * NQ + s])
                q = QST[0:ROWS, i % 2, (s % 8) * 4 + s // 8, :]
                kk = ((s // 2) % 8) * 2 + (s // 2) // 8
                for a in range(0, w, 512):
                    n = min(512, w - a)
                    last = a + n == w
                    pe.matmul(SP_[:, k[a // 512], 0:n], q, KST[0:ROWS, a // P:(a + n) // P, kk, :], start=True, stop=not last)
                ins = pe.matmul(SP_[:, k[(w - P) // 512], (w - P) % 512:(w - P) % 512 + P], identb[:, :], maskb[:, :],
                                start=False, stop=True)
                ins.then_inc(s_ready, 1)

            def diff_transposes(b, i, n, g):
                u = i * H + n
                after(pe, d_ready, b * N_U + u + 1)
                after(pe, dt_ready, b * N_T + tg(i, n, g))
                for k in range(4 * g, min(4 * g + 4, i + 1)):
                    ins = pe.transpose(DP[:, P * (k - 4 * g):P * (k - 4 * g + 1)], E1[:, u % 2, P * k:P * (k + 1)], ident[:, :])
                ins.then_inc(t_ready, 1)

            def diff_v(b, i, u, g):
                after(pe, dt_ready, b * N_T + tg(i, HALF * u + HALF - 1, g) + 1)
                if u == 0 and g == 0:
                    after(pe, at_ready, b * TILES + i)
                    if i == 0:
                        after(pe, v0_moved, b + 1)
                    else:
                        after(pe, kv_roped, b * TILES + i + 1)
                for k in range(4 * g, min(4 * g + 4, i + 1)):
                    for q in range(4):
                        v = DV * (4 * u + q)
                        ins = pe.matmul(PV[DV * q:DV * (q + 1), 2 * P * u:2 * P * (u + 1)], V[:, k, v:v + DV],
                                        DT[:, k, 2 * q:2 * q + 2, :], start=(k == 0), stop=(k == i), skip_group_check=True)
                ins.then_inc(pv_done, 1)

            def attention(T, s, h):
                b, t = T.b, T.t
                old = T.before(s - 1) if h else T.before(s - 2)
                ended = T.before(s - 2 - (1 - h))
                if h and T.attend and t >= 4:
                    scores(b, t, 2 * s + 1)
                if ended and ended[2] % HALF == HALF - 1 and 1 - h < groups(ended[1]):
                    diff_v(ended[0], ended[1], ended[2] // HALF, 1 - h)
                if old and 1 - h < groups(old[1]):
                    diff_transposes(*old, 1 - h)
                if h == 0 and T.attend:
                    scores(b, t, 2 * s)
                    if t < 4:
                        scores(b, t, 2 * s + 1)

            def first_product(T, k, j):
                f = 2 * k + j
                if j == 0:
                    hold(pe, x2_ready, 2 * T.pair + 2)
                    if k == 0:
                        hold(pe, o_sum, 2 * T.pair)
                    else:
                        hold(pe, hp_ready, 8 * T.pair + k)
                for c in range(KD):
                    for xp in (X2H, X2L):
                        ins = pe.matmul(F[:, 2 * P * j:2 * P * (j + 1)], W1Q[:, c, P * f:P * (f + 1)], xp[:, c, :],
                                        start=(c == 0 and xp is X2H), stop=(c == KD - 1 and xp is X2L))
                if j == 1:
                    ins.then_inc(f1_ready, 1)

            def second_product(q, j, f):
                if f == 0:
                    if j == 0:
                        hold(pe, hp_ready, 8 * q + 8)
                    else:
                        hold(pe, o_sum, 2 * q + 1)
                if j == 0 and f % 2 == 0:
                    hold(pe, h_ready, 8 * q + f // 2 + 1)
                for hp in (HH, HL):
                    ins = pe.matmul(F[:, :], hp[:, f, P * j:P * (j + 1)], W2Q[:, f, :],
                                    start=(f == 0 and hp is HH), stop=(f == FT - 1 and hp is HL))
                if f == FT - 1:
                    ins.then_inc(f2_ready, 1)

            def pe_work(T):
                b, t, nb, nf = T.b, T.t, T.nb, T.nf
                for hs in range(HS_TILE):
                    attention(T, *divmod(hs, 2))
                    if T.attend:
                        if hs == LN1_TURN:
                            after(pe, xn_ready, nb + 1)
                            after(pe, rest_part, 2 * nb)
                            after(pe, x2_ready, nf)
                            transposes(TOK, KD, m_xt)
                        if hs == Q_PROJ:
                            after(pe, xt_ready, nb + 1)
                        if Q_PROJ <= hs < Q_PROJ + 3:
                            project(WQKV, 0, ((0,), (1,), (2, 3))[hs - Q_PROJ], m_q)
                    if T.finish and hs == AT_TURN:
                        if T.attend:
                            after(pe, q_roped, nb + 1)
                        after(pe, x2_ready, nf)
                        after(pe, at_ready, nf + 1)
                        transposes(AT, KD, m_at)
                    if T.attend:
                        if hs == KV_PROJ:
                            after(pe, q_roped, nb + 1)
                            if T.finish:
                                after(pe, attn_ready, nf + 1)
                        if KV_PROJ <= hs < KV_PROJ + 3:
                            project(WQKV, D, ((0,), (1,), (2, 3))[hs - KV_PROJ], m_kv)
                        if hs == Q_TURN:
                            after(pe, kv_roped, nb + 1)
                            after(pe, rope_sum, 2 * nb + 1)
                            transposes(T1, KD, m_qt)
                        if hs == K_TURN:
                            after(pe, rest_part, 2 * nb + 1)
                            after(pe, rope_sum, 2 * nb + 2)
                            transposes(T1[:, D:D + DKV], 2, m_kt)
                    if T.finish:
                        if hs == AN_TURN:
                            if T.attend:
                                after(pe, rest_part, 2 * nb + 2)
                            after(pe, an_ready, nf + 1)
                            transposes(TOK, KD, m_ant)
                        if hs == O_PROJ:
                            after(pe, ant_ready, nf + 1)
                        if O_PROJ <= hs < O_PROJ + 3:
                            project(WO, 0, ((0,), (1,), (2, 3))[hs - O_PROJ], m_wo)
                        if hs == LN2_TURN:
                            after(pe, x1_ready, nf + 1)
                            after(pe, xn2_ready, nf + 1)
                            transposes(TOK, KD, m_x2t)
                    piece = T.first_piece(hs)
                    if piece:
                        first_product(T, *piece)
                    if T.w1b and hs >= W2_ODD:
                        second_product(T.pair, 0, hs - W2_ODD)
                    if T.w2b and W2_EVEN <= hs < W2_EVEN + FT:
                        second_product(T.pair - 1, 1, hs - W2_EVEN)

            pe.wait_ge(xn_ready, 1)
            transposes(TOK, KD, m_xt)
            pe.wait_ge(xt_ready, 1)
            pe.wait_ge(ready, 5)
            project(WQKV, 0, range(KD), m_q)
            pe.wait_ge(q_roped, 1)
            project(WQKV, D, range(KD), m_kv)
            pe.wait_ge(kv_roped, 1)
            pe.wait_ge(rope_sum, 1)
            transposes(T1, KD, m_qt)
            pe.wait_ge(rest_part, 1)
            pe.wait_ge(rope_sum, 2)
            transposes(T1[:, D:D + DKV], 2, m_kt)
            every_block(pe, pe_work)


def rope_tables():
    inv = (np.float32(ROPE_THETA) ** (-np.arange(DH, dtype=np.float32) / np.float32(DH))).astype(np.float32)
    f = (np.arange(S, dtype=np.float32)[:, None] * inv[None, :]).astype(np.float32)
    cos, sin = np.cos(f).astype(np.float32), np.sin(f).astype(np.float32)
    sin[:, :DH // 2] *= -1
    t = np.stack([cos, sin])
    return np.ascontiguousarray(t.reshape(2, TILES, P, DH).transpose(2, 0, 1, 3))


def kernel(**inputs):
    import numpy as _np
    import concourse.bacc as _bacc
    from concourse import mybir as _mybir
    from concourse.bass_utils import run_bass_kernel_spmd as _run

    nc = _bacc.Bacc("TRN2", target_bir_lowering=False, num_devices=1)
    a = {k: _np.asarray(v) for k, v in inputs.items()}
    x = a["L0_attn_hidden_states"]
    arrays = {
        "x": _np.concatenate([x, x[:1]], axis=0),
        "wqT": a["L0_attn_Wq"].T, "wkT": a["L0_attn_Wk"].T, "wvT": a["L0_attn_Wv"].T,
        "woT": a["L0_attn_Wo"].T.reshape(2, 4, 2, DV, D).transpose(0, 2, 1, 3, 4).reshape(KD, P, D),
        "lams": _np.stack([a["L0_attn_lambda_q1"], a["L0_attn_lambda_k1"], a["L0_attn_lambda_q2"], a["L0_attn_lambda_k2"]]),
        "subw": a["L0_attn_subln_weight"],
        "w1T": a["L0_ffn_w1"].T, "b1": a["L0_ffn_b1"].reshape(FT, P).T,
        "w2T": a["L0_ffn_w2"].T, "b2": a["L0_ffn_b2"],
        "rope": rope_tables(),
    }
    feeds, args = {}, []
    for name, v in arrays.items():
        v = _np.ascontiguousarray(v)
        feeds[f"in_{name}"] = v
        args.append(nc.dram_tensor(f"in_{name}", v.shape, _mybir.dt.from_np(v.dtype), kind="ExternalInput").ap())
    args.append(nc.dram_tensor("out_0", (B, S, D), F32, kind="ExternalOutput").ap())
    diff_attention_ffn(nc, *args)
    r = _run(nc, [feeds], core_ids=[0])
    return r.results[0]["out_0"]
```

```python
import math
from contextlib import ExitStack

import numpy as np

import concourse.bass as bass
from concourse import mybir

F32 = mybir.dt.float32
F16 = mybir.dt.float16
BF16 = mybir.dt.bfloat16
F8 = mybir.dt.float8e4
ALU = mybir.AluOpType
ACT = mybir.ActivationFunctionType
AX = mybir.AxisListType

P = 128
B, S, D = 8, 1024, 512
H, KVH = 16, 8
DH = D // H // 2
DV = 2 * DH
NQ, NK = 2 * H, 2 * KVH
DKV = NK * DH
FF = 2048
KD = D // P
FT = FF // P
TILES = S // P
HALF = H // 2
EPS = 1e-5
LAMBDA_INIT = 0.8 - 0.6 * math.exp(-0.3 * 2)
ROPE_THETA = 10000.0
TERNARY_CUT = 0.7
MASKED = -1e30
XS = 2048.0
HS = 1.0 / 16
PROD = 6
QPART = (0, 0, 0, 1, 1, 2)
KPART = (0, 1, 2, 0, 1, 0)
ROWS = PROD * DH
GELU_F = FT // 2
HS_TILE = 2 * H



def groups(i):
    return 1 if i < 4 else 2


def tg(i, n, g):
    return (H * i if i < 4 else H * 4 + 2 * H * (i - 4)) + n * groups(i) + g


def pg(i, u, g):
    return (2 * i if i < 4 else 8 + 4 * (i - 4)) + u * groups(i) + g


def banks(i, s):
    return [s % 4] if i < 4 else [2 * (s % 2), 2 * (s % 2) + 1]



def slot_users():
    last = {0: -1, 1: -1, 2: 0, 3: 0}
    need = []
    for i in range(TILES):
        for s in range(NQ):
            need.append(max([last[k] for k in banks(i, s)]))
            for k in banks(i, s):
                last[k] = i * NQ + s + 1
    return need


SLOT_FREE = slot_users()
N_T = tg(TILES - 1, H - 1, 1) + 1
N_PV = pg(TILES - 1, 1, 1) + 1
N_E = NQ * TILES
N_U = H * TILES

LN1_STATS, LN1_ROWS, LN1_TURN = 1, 3, 4
Q_PROJ, Q_ROPE = (7, 8, 9, 10), 11
KV_PROJ, KV_ROPE = (12, 13, 14, 14), 15
Q_TURN, Q_REST, K_TURN, K_REST = 16, 17, 20, 21
V0_MOVE = 5
PV_OUT = (19, 3)
AT_TURN, AT_ROWS = 6, 6
MEAN_SQ, RMS_ROWS, AN_TURN = 9, 13, 22
O_PROJ, O_SUM = (23, 24, 25, 26), 27
LN2_STATS, LN2_ROWS, LN2_TURN, LN2_REST = 27, 29, 30, 31
W1_AT = (1, 4, 7, 10, 13, 16, 19, 22)
GELU = (13, 25)
SPLIT_AT = (14, 16, 17, 18, 26, 27, 28, 29)
W2_AT, W2_N = (3, 18), 13
OUT_AT = (17, 31)


class QBlock:

    def __init__(self, b, t, kind):
        def runs(start, ends):
            return kind == "loop" or (kind == "first" and t >= start) or (kind == "last" and t in ends)

        self.b, self.t = b, t
        self.attend = kind != "last"
        self.finish = runs(1, (0,))
        self.w1 = t % 2 == 1 and runs(3, (1,))
        self.w2 = t % 2 == 0 and runs(4, (0, 2))
        self.nb = b * TILES + t + 1
        self.nf = b * TILES + t - 1
        self.pair = b * (TILES // 2) + t // 2 - (1 if t % 2 else 2)
        self.no = b * TILES + t - (3 if t % 2 else 4)
        self.next = (t + 1) % TILES

    def before(self, n):
        if n >= 0:
            return (self.b, self.t, n) if self.attend else None
        if not self.finish:
            return None
        return (self.b, self.t - 1, n + H) if self.t else (self.b - 1, TILES - 1, n + H)

    def first_product(self, hs):
        for k, at in enumerate(W1_AT if self.w1 else ()):
            if hs in (at, at + 1, at + 2):
                return k, hs - at
        return None

    def second_product(self, hs):
        for j, at in enumerate(W2_AT if self.w2 else ()):
            if at <= hs < at + W2_N:
                return j, range(FT * (hs - at) // W2_N, FT * (hs - at + 1) // W2_N)
        return None


def every_block(eng, run):
    for t in range(TILES):
        run(QBlock(0, t, "first"))
    with eng.Fori(1, B) as b:
        for t in range(TILES):
            run(QBlock(b, t, "loop"))
    for t in range(3):
        run(QBlock(B, t, "last"))


def diff_attention_ffn(nc, x, wqT, wkT, wvT, woT, lams, subw, w1T, b1, w2T, b2, rope, out):
    ctx = ExitStack()
    with ctx:
        def sb(name, shape, dt):
            return ctx.enter_context(nc.sbuf_tensor(name, shape, dt))

        def sem(name):
            return ctx.enter_context(nc.semaphore(name))

        WQKV = sb("WQKV", [P, KD, D + 2 * DKV], F32)
        WO = sb("WO", [P, KD, D], F32)
        W1Q = sb("W1Q", [P, KD, FF], F8)
        W2Q = sb("W2Q", [P, FT, D], F8)
        ident = sb("ident", [P, P], F32)
        identb = sb("identb", [P, P], BF16)
        maskb = sb("maskb", [P, P], BF16)
        nhalf = sb("nhalf", [P, H], F32)
        ropet = sb("ropet", [P, 2, TILES, DH], F32)
        b1c = sb("b1c", [P, FT], F32)
        b2b = sb("b2b", [P, D], F32)
        subc = sb("subc", [P, 1], F32)
        lamt = sb("lamt", [P, 4, DH], F32)
        lamp = sb("lamp", [P, 2, DH], F32)
        lams2 = sb("lams2", [P, 2], F32)
        lame = sb("lame", [P, 2], F32)
        neglam = sb("neglam", [P, 1], F32)
        wtot = sb("wtot", [P, 2], F32)
        thr = sb("thr", [P, 2, 2], F32)
        KST = sb("KST", [P, TILES, NK, P], BF16)
        QST = sb("QST", [P, 2, NQ, P], BF16)
        V = sb("V", [P, TILES, DKV], F32)
        E1 = sb("E1", [P, 2, S], F32)
        E2 = sb("E2", [P, S], F32)
        DT = sb("DT", [P, TILES, HALF, P], F32)
        NM = sb("NM", [P, 8], F32)
        SUM = sb("SUM", [P, 2, 2, H], F32)
        RS = sb("RS", [P, 2, 2, H], F32)
        CC = sb("CC", [P, 2], F32)
        VST = sb("VST", [P, DKV], F32)
        X = sb("X", [P, 4, D], F32)
        TOK = sb("TOK", [P, D], F32)
        WT = sb("WT", [P, D], F32)
        ST = sb("ST", [P, 6], F32)
        MV = sb("MV", [P, 2], F32)
        VE = sb("VE", [P, H], F32)
        RST = sb("RST", [P, H], F32)
        T1 = sb("T1", [P, D + DKV], F32)
        T2 = sb("T2", [P, D + DKV], F32)
        SPL = sb("SPL", [P, 3, D + DKV], BF16)
        AT = T1
        SQ = sb("SQ", [P, D], F32)
        MS = sb("MS", [P, H], F32)
        X1 = sb("X1", [P, 4, D], F32)
        X2H = sb("X2H", [P, KD, 2 * P], F16)
        X2L = sb("X2L", [P, KD, 2 * P], F16)
        HP = sb("HP", [P, GELU_F, 2 * P], F32)
        HH = sb("HH", [P, FT, 2 * P], F16)
        HL = sb("HL", [P, FT, 2 * P], F16)
        OUT = SQ

        SP_ = ctx.enter_context(nc.psum_tensor("SP_", [P, 4, 512], F32))
        DP = ctx.enter_context(nc.psum_tensor("DP", [P, 512], F32))
        DX = ctx.enter_context(nc.psum_tensor("DX", [P, 512], F32))
        M = ctx.enter_context(nc.psum_tensor("M", [P, 512], F32))
        F = ctx.enter_context(nc.psum_tensor("F", [P, 512], F32))

        scratch = nc.dram_tensor("scratch", [2, P, 3, D + DKV], BF16, kind="Internal").ap()

        qkv_in = sem("qkv_in")
        w_in = sem("w_in")
        w1_in = sem("w1_in")
        w2_in = sem("w2_in")
        pool_const = sem("pool_const")
        lam_prod = sem("lam_prod")
        lam_exp = sem("lam_exp")
        set_chain = sem("set_chain")
        abs_sum = sem("abs_sum")
        abs_all = sem("abs_all")
        wq_scaled = sem("wq_scaled")
        w1_cut = sem("w1_cut")
        ready = sem("ready")
        x_in = [sem("x_in_even"), sem("x_in_odd")]
        ln_chain = [sem("ln1_chain"), sem("ln2_chain")]
        ln_var = [sem("ln1_var"), sem("ln2_var")]
        ln_rstd = [sem("ln1_rstd"), sem("ln2_rstd")]
        xn_ready = sem("xn_ready")
        m_xt = sem("m_xt")
        xt_ready = sem("xt_ready")
        m_q = sem("m_q")
        q_roped = sem("q_roped")
        m_kv = sem("m_kv")
        kv_roped = sem("kv_roped")
        v0_moved = sem("v0_moved")
        rope_sum = sem("rope_sum")
        m_qt = sem("m_qt")
        m_kt = sem("m_kt")
        high_part = sem("high_part")
        rest_part = sem("rest_part")
        mid_part = sem("mid_part")
        split_done = sem("split_done")
        scr_out = sem("scr_out")
        stacked = sem("stacked")
        s_ready = sem("s_ready")
        max_ready = sem("max_ready")
        exp_done = sem("exp_done")
        d_chain = sem("d_chain")
        d_ready = sem("d_ready")
        t_ready = sem("t_ready")
        dt_ready = sem("dt_ready")
        pv_done = sem("pv_done")
        at_ready = sem("at_ready")
        m_at = sem("m_at")
        attn_ready = sem("attn_ready")
        sq_ready = sem("sq_ready")
        ms_chain = sem("ms_chain")
        ms_ready = sem("ms_ready")
        rms_ready = sem("rms_ready")
        an_ready = sem("an_ready")
        m_ant = sem("m_ant")
        ant_ready = sem("ant_ready")
        m_wo = sem("m_wo")
        x1_ready = sem("x1_ready")
        xn2_ready = sem("xn2_ready")
        m_x2t = sem("m_x2t")
        x2h_ready = sem("x2h_ready")
        x2_ready = sem("x2_ready")
        f1_ready = sem("f1_ready")
        hp_ready = sem("hp_ready")
        gelu_done = sem("gelu_done")
        h_chain = sem("h_chain")
        h_ready = sem("h_ready")
        f2_ready = sem("f2_ready")
        o_sum = sem("o_sum")
        o_ready = sem("o_ready")
        o_out = sem("o_out")
        held = sem("held")

        onesf = E1[:, 0, 0:P]
        wsum = E1[:, 1, 0:2 * 64].rearrange("p (a b) -> p a b", b=64)
        w1f = KST[:, :, :, :].rearrange("p a b c -> p (a b c)").bitcast(F32)
        w2f = DT[:, :, :, :].rearrange("p a b c -> p (a b c)")
        cutt = HP[:, :, :].rearrange("p a b -> p (a b)")

        def hold(eng, signal, value):
            if not isinstance(value, int) or value > 0:
                eng.wait_ge(signal, value)
                eng.sem_inc(held, 1)

        def after(eng, signal, value):
            if not isinstance(value, int) or value > 0:
                eng.wait_ge(signal, value)

        def score_out(i, s, w):
            k = banks(i, s)
            return SP_[:, k[0]:k[0] + len(k), :].rearrange("p a b -> p (a b)")[:, 0:w]

        def qk3(ap):
            return ap.rearrange("p (s d) -> p s d", d=DH)

        block = ctx.enter_context(nc.Block())

        @block.sync
        def _(sp):
            for j in range(2):
                sp.dma_start(X[:, j, :], x[0, j * P:(j + 1) * P, :]).then_inc(x_in[j], 16)
            sp.dma_start(WQKV[:, :, 0:D], wqT.rearrange("(k p) n -> p k n", p=P)).then_inc(qkv_in, 16)
            sp.dma_start(WQKV[:, :, D:D + DKV], wkT.rearrange("(k p) n -> p k n", p=P)).then_inc(qkv_in, 16)
            sp.dma_start(WQKV[:, :, D + DKV:D + 2 * DKV], wvT.rearrange("(k p) n -> p k n", p=P)).then_inc(qkv_in, 16)
            sp.dma_start(ropet[:, :, :, :], rope).then_inc(qkv_in, 16)
            sp.dma_start(w1f.rearrange("p (k n) -> p k n", k=KD), w1T.rearrange("(k p) n -> p k n", p=P)).then_inc(w1_in, 16)
            sp.dma_start(w2f.rearrange("p (k n) -> p k n", k=FT), w2T.rearrange("(k p) n -> p k n", p=P)).then_inc(w2_in, 16)
            sp.dma_start(WO[:, :, :], woT.rearrange("k p n -> p k n")).then_inc(w_in, 16)
            sp.dma_start(b1c[:, :], b1).then_inc(w_in, 16)
            sp.dma_start(b2b[:, :], b2.partition_broadcast(P)).then_inc(w_in, 16)
            for j in range(4):
                sp.dma_start(lamt[:, j, :], lams[j].partition_broadcast(P)).then_inc(w_in, 16)
                sp.dma_start(subc[DV * j:DV * (j + 1), :], subw.unsqueeze(1)).then_inc(w_in, 16)

            def stack(nb, tile, q_free, k_free):
                hold(sp, stacked, 16 * 2 * PROD * (nb - 1))
                hold(sp, split_done, 2 * nb + 2)
                sp.dma_start(scratch[tile % 2], SPL[:, :, :]).then_inc(scr_out, 16)
                hold(sp, scr_out, 16 * nb + 16)
                src = scratch[tile % 2].rearrange("(s d) a (c n) -> a d s c n", d=DH, n=P)
                hold(sp, s_ready, q_free)
                for j in range(PROD):
                    sp.dma_start(QST[DH * j:DH * (j + 1), tile % 2, :, :].rearrange("p (s c) n -> p s c n", s=8),
                                 src[QPART[j], :, :, 0:4, :]).then_inc(stacked, 16)
                if k_free is not None:
                    hold(sp, s_ready, k_free)
                for j in range(PROD):
                    sp.dma_start(KST[DH * j:DH * (j + 1), tile, :, :].rearrange("p (s c) n -> p s c n", s=8),
                                 src[KPART[j], :, :, 4:6, :]).then_inc(stacked, 16)

            def result(T, j):
                k = T.t - 4 + j
                hold(sp, o_ready, T.no + j + 1)
                rows = out[T.b, k * P:(k + 1) * P, :] if k >= 0 else out[T.b - 1, (k + 8) * P:(k + 9) * P, :]
                sp.dma_start(rows, OUT[:, :]).then_inc(o_out, 16)

            def dma_work(T):
                b, t = T.b, T.t
                if T.attend:
                    j = (t + 2) % TILES
                    hold(sp, x1_ready, T.nf)
                    row = x[b] if t < TILES - 2 else x[b + 1]
                    sp.dma_start(X[:, j % 4, :], row[j * P:(j + 1) * P, :]).then_inc(x_in[t % 2], 16)
                if T.w2:
                    result(T, 0)
                if T.attend:
                    stack(T.nb, T.next, b * N_E + t * NQ, (b + 1) * N_E if t == TILES - 1 else None)
                if T.w2:
                    result(T, 1)

            sp.wait_ge(w1_cut, 1)
            stack(0, 0, 0, None)
            every_block(sp, dma_work)
            sp.wait_ge(o_out, 16 * B * TILES)
            sp.wait_ge(x_in[0], 16 * (B * TILES // 2 + 1))
            sp.wait_ge(x_in[1], 16 * (B * TILES // 2 + 1))
            sp.wait_ge(stacked, 16 * 2 * PROD * (B * TILES + 1))

        @block.gpsimd
        def _(pool):
            pool.memset(ident[:, :], 0.0).then_inc(pool_const, 1)
            pool.memset(identb[:, :], 0.0).then_inc(pool_const, 1)
            pool.memset(maskb[:, :], 0.0).then_inc(pool_const, 1)
            pool.memset(onesf, 1.0).then_inc(pool_const, 1)
            pool.memset(nhalf[:, :], -0.5).then_inc(pool_const, 1)
            pool.wait_ge(pool_const, 5)
            for m in (ident, identb):
                pool.affine_select(out=m[:, :], in_=m[:, :], compare_op=ALU.not_equal, fill=1.0,
                                   base=0, pattern=[[-1, P]], channel_multiplier=1).then_inc(pool_const, 1)
            pool.affine_select(out=maskb[:, :], in_=maskb[:, :], compare_op=ALU.is_ge, fill=MASKED,
                               base=0, pattern=[[-1, P]], channel_multiplier=1).then_inc(pool_const, 1)
            pool.wait_ge(pool_const, 8)

            def rstd(j, n):
                after(pool, ln_var[j], n + 1)
                pool.tensor_tensor(RST[:, 0:1], VE[:, 0:1], nhalf[:, 0:1], ALU.pow).then_inc(ln_rstd[j], 1)

            def rope_add(nb, part):
                c = slice(0, D) if part == 0 else slice(D, D + DKV)
                after(pool, q_roped if part == 0 else kv_roped, nb + 1)
                pool.tensor_tensor(T1[:, c], T1[:, c], T2[:, c], ALU.add).then_inc(rope_sum, 1)

            def split(nb, part):
                c = slice(0, D) if part == 0 else slice(D, D + DKV)
                hold(pool, rest_part, 2 * nb + part + 1)
                pool.tensor_scalar(SPL[:, 1, c], T2[:, c], 1.0, 0.0, ALU.mult, ALU.add).then_inc(mid_part, 1)
                after(pool, mid_part, 2 * nb + part + 1)
                pool.tensor_tensor(SPL[:, 2, c], T2[:, c], SPL[:, 1, c], ALU.subtract).then_inc(split_done, 1)

            def hidden_split(q, k):
                n = 8 * q + k
                h = slice(2 * k % GELU_F, 2 * k % GELU_F + 2)
                fs = slice(2 * k, 2 * k + 2)
                after(pool, gelu_done, 2 * q + k // 4 + 1)
                hold(pool, f2_ready, 2 * q)
                pool.tensor_scalar(HH[:, fs, :], HP[:, h, :], HS, 0.0, ALU.mult, ALU.add).then_inc(h_chain, 1)
                hold(pool, h_chain, 2 * n + 1)
                pool.tensor_scalar(HP[:, h, :], HP[:, h, :], HS, 0.0, ALU.mult, ALU.add).then_inc(h_chain, 1)
                after(pool, h_chain, 2 * n + 2)
                pool.tensor_tensor(HL[:, fs, :], HP[:, h, :], HH[:, fs, :], ALU.subtract).then_inc(h_ready, 1)

            def pool_work(T):
                for hs in range(HS_TILE):
                    if T.attend:
                        if hs == LN1_STATS:
                            rstd(0, T.nb)
                        if hs == V0_MOVE and T.t == 0:
                            hold(pool, pv_done, T.b * N_PV)
                            hold(pool, kv_roped, T.nb)
                            pool.tensor_copy(V[:, 0, :], VST[:, :]).then_inc(v0_moved, 1)
                        if hs == Q_ROPE:
                            rope_add(T.nb, 0)
                        if hs == KV_ROPE:
                            rope_add(T.nb, 1)
                    if T.finish:
                        if hs == AT_ROWS:
                            after(pool, attn_ready, T.nf + 1)
                            after(pool, o_out, 16 * T.no)
                            pool.tensor_tensor(SQ[:, :], TOK[:, :], TOK[:, :], ALU.mult).then_inc(sq_ready, 1)
                        if hs == MEAN_SQ:
                            after(pool, ms_ready, T.nf + 1)
                            pool.tensor_tensor(RST[:, :], VE[:, :], nhalf[:, :], ALU.pow).then_inc(rms_ready, 1)
                        if hs == RMS_ROWS:
                            tok = TOK[:, :].rearrange("p (c d) -> p c d", d=DV)
                            after(pool, rms_ready, T.nf + 1)
                            pool.tensor_tensor(tok, tok, RST[:, :].unsqueeze(2).broadcast_to([P, H, DV]),
                                               ALU.mult).then_inc(an_ready, 1)
                        if hs == LN2_STATS:
                            rstd(1, T.nf)
                    if T.attend and hs == Q_REST:
                        split(T.nb, 0)
                    if T.attend and hs == K_REST:
                        split(T.nb, 1)
                    if T.w1 and hs in SPLIT_AT:
                        hidden_split(T.pair, SPLIT_AT.index(hs))
                    if T.w2 and hs in OUT_AT:
                        after(pool, o_sum, T.no + OUT_AT.index(hs) + 1)
                        pool.tensor_tensor(OUT[:, :], OUT[:, :], b2b[:, :], ALU.add).then_inc(o_ready, 1)

            rstd(0, 0)
            rope_add(0, 0)
            rope_add(0, 1)
            split(0, 0)
            split(0, 1)
            every_block(pool, pool_work)

        @block.scalar
        def _(act):
            def xt_copy(nb, wo_done):
                after(act, m_xt, nb + 1)
                after(act, m_wo, wo_done)
                act.activation(WT[:, :], M[:, :], ACT.Copy).then_inc(xt_ready, 1)

            def high(nb, part):
                c, n = (slice(0, D), D) if part == 0 else (slice(D, D + DKV), DKV)
                after(act, m_qt if part == 0 else m_kt, nb + 1)
                if part == 0:
                    after(act, scr_out, 16 * nb)
                act.activation(SPL[:, 0, c], M[:, 0:n], ACT.Copy).then_inc(high_part, 1)

            def exp(T, n, k):
                b, i = T.b, T.t
                u = i * H + n
                w = P * (i + 1)
                after(act, max_ready, b * N_E + 2 * u + k + 1)
                if k == 0:
                    old = T.before(n - 2)
                    if old:
                        pb, pi, pn = old
                        after(act, t_ready, pb * N_T + tg(pi, pn, groups(pi) - 1) + 1)
                    dst = E1[:, u % 2, 0:w]
                else:
                    after(act, d_ready, b * N_U + u - (1 if i < 4 and u > 0 else 0))
                    e = 512 * (u % 2) if i < 4 else 0
                    dst = E2[:, e:e + w]
                col = 8 * (n // 8) + 4 * (n % 2) + (n % 8) // 2
                act.activation(dst, score_out(i, 2 * n + k, w), ACT.Exp, bias=NM[:, (2 * u + k) % 8:(2 * u + k) % 8 + 1],
                               scale=1.0, accum_out=SUM[:, i % 2, k, col:col + 1]).then_inc(exp_done, 1)

            def dt_copy(b, i, n, g):
                k0, k1 = 4 * g, min(4 * g + 4, i + 1)
                after(act, t_ready, b * N_T + tg(i, n, g) + 1)
                if n % HALF == 0:
                    if n or i:
                        pi, pu = (i, 0) if n else (i - 1, 1)
                        after(act, pv_done, b * N_PV + pg(pi, pu, min(g, groups(pi) - 1)) + 1)
                    else:
                        after(act, pv_done, b * N_PV - 1)
                act.activation(DT[:, k0:k1, n % HALF, :], (DP, DX)[g][:, 0:P * (k1 - k0)].rearrange("p (k q) -> p k q", q=P),
                               ACT.Copy).then_inc(dt_ready, 1)

            def act_work(T):
                t, nb, nf = T.t, T.nb, T.nf
                for hs in range(HS_TILE):
                    s, h = divmod(hs, 2)
                    old = T.before(s - 1) if h else T.before(s - 2)
                    if T.attend:
                        exp(T, s, h)
                    if old and (h == 1 or groups(old[1]) == 2):
                        dt_copy(*old, 1 - h)
                    if T.attend and hs == LN1_TURN:
                        xt_copy(nb, nf)
                    if T.attend and hs == PV_OUT[0]:
                        after(act, pv_done, T.b * N_PV + pg(t, 0, groups(t) - 1) + 1)
                        after(act, m_qt, nb + 1)
                        act.activation(AT[:, 0:2 * P], M[:, 0:2 * P], ACT.Copy).then_inc(at_ready, 1)
                    if T.finish and hs == PV_OUT[1]:
                        pb, pi, _ = T.before(-1)
                        after(act, pv_done, pb * N_PV + pg(pi, 1, groups(pi) - 1) + 1)
                        act.activation(AT[:, 2 * P:4 * P], M[:, 0:2 * P], ACT.Copy).then_inc(at_ready, 1)
                    if T.attend and hs == Q_TURN:
                        high(nb, 0)
                    if T.attend and hs == K_TURN:
                        high(nb, 1)
                    if T.finish and hs == AN_TURN:
                        after(act, m_ant, nf + 1)
                        if T.attend:
                            after(act, m_kv, nb + 1)
                        act.activation(WT[:, :], M[:, :], ACT.Copy).then_inc(ant_ready, 1)
                    if T.finish and hs == LN2_TURN:
                        after(act, m_x2t, nf + 1)
                        if t % 2:
                            after(act, f1_ready, 8 * (T.pair + 1))
                        act.activation(X2H[:, :, P * ((t - 1) % 2):P * ((t - 1) % 2) + P],
                                       M[:, :].rearrange("p (k n) -> p k n", k=KD), ACT.Copy, scale=XS).then_inc(x2h_ready, 1)
                    piece = T.first_product(hs)
                    if piece and piece[1] == 2:
                        k, n = piece[0], 8 * T.pair + piece[0]
                        after(act, f1_ready, n + 1)
                        after(act, h_ready, n - 3)
                        for f in (2 * k, 2 * k + 1):
                            ins = act.activation(HP[:, f % GELU_F, :], F[:, 2 * P * (f % 2):2 * P * (f % 2) + 2 * P],
                                                 ACT.Identity, bias=b1c[:, f:f + 1], scale=1.0 / XS)
                        ins.then_inc(hp_ready, 1)
                    if T.w1 and hs in GELU:
                        j = GELU.index(hs)
                        after(act, hp_ready, 8 * T.pair + 4 * j + 4)
                        act.activation(HP[:, :, :], HP[:, :, :], ACT.Gelu).then_inc(gelu_done, 1)

            xt_copy(0, 0)
            high(0, 0)
            high(0, 1)
            act.wait_ge(lam_prod, 1)
            act.activation(lame[:, :], lams2[:, :], ACT.Exp).then_inc(lam_exp, 1)
            every_block(act, act_work)

        @block.vector
        def _(dve):
            setup = [0]

            def link(ins):
                setup[0] += 1
                ins.then_inc(set_chain, 1)
                dve.wait_ge(set_chain, setup[0])

            def variance(j, src, n):
                nc.vector.bn_stats(ST[:, :], src).then_inc(ln_chain[j], 1)
                hold(dve, ln_chain[j], 2 * n + 1)
                nc.vector.bn_aggr(MV[:, :], ST[:, :]).then_inc(ln_chain[j], 1)
                after(dve, ln_chain[j], 2 * n + 2)
                nc.vector.tensor_scalar(VE[:, 0:1], MV[:, 1:2], EPS, None, ALU.add).then_inc(ln_var[j], 1)

            def normalise(j, src, n, done):
                after(dve, ln_rstd[j], n + 1)
                nc.vector.tensor_scalar(TOK[:, :], src, MV[:, 0:1], RST[:, 0:1], ALU.subtract, ALU.mult).then_inc(done, 1)

            def rope_mul(nb, tile, part, moved=0):
                full, c0, n = (m_q, 0, NQ) if part == 0 else (m_kv, D, NK)
                after(dve, full, nb + 1)
                if part == 0:
                    after(dve, m_kt, nb)
                    after(dve, split_done, 2 * nb)
                src = qk3(M[:, 0:n * DH])
                d1, d2 = qk3(T1[:, c0:c0 + n * DH]), qk3(T2[:, c0:c0 + n * DH])
                hd = DH // 2
                cos = ropet[:, 0, tile, :].unsqueeze(1).broadcast_to([P, n, DH])
                sn1 = ropet[:, 1, tile, 0:hd].unsqueeze(1).broadcast_to([P, n, hd])
                sn2 = ropet[:, 1, tile, hd:DH].unsqueeze(1).broadcast_to([P, n, hd])
                nc.vector.tensor_tensor(d1, src, cos, ALU.mult)
                nc.vector.tensor_tensor(d2[:, :, 0:hd], src[:, :, hd:DH], sn1, ALU.mult)
                ins = nc.vector.tensor_tensor(d2[:, :, hd:DH], src[:, :, 0:hd], sn2, ALU.mult)
                if part == 0:
                    ins.then_inc(q_roped, 1)
                else:
                    if tile == 0:
                        after(dve, v0_moved, moved)
                    v = V[:, tile, :] if tile else VST[:, :]
                    nc.vector.tensor_copy(v, M[:, DKV:2 * DKV]).then_inc(kv_roped, 1)

            def rest(nb, part):
                c, n = (slice(0, D), D) if part == 0 else (slice(D, D + DKV), DKV)
                after(dve, high_part, 2 * nb + part + 1)
                nc.vector.tensor_tensor(T2[:, c], M[:, 0:n], SPL[:, 0, c], ALU.subtract).then_inc(rest_part, 1)

            def row_max(b, i, n, k):
                m = (2 * (i * H + n) + k) % 8
                after(dve, s_ready, b * N_E + i * NQ + 2 * n + k + 1)
                nc.vector.tensor_reduce(NM[:, m:m + 1], score_out(i, 2 * n + k, P * (i + 1)), AX.X, ALU.max,
                                        negate=True).then_inc(max_ready, 1)

            def row_max_pair(b, i, n):
                m = (2 * (i * H + n)) % 8
                k = banks(i, 2 * n)[0]
                after(dve, s_ready, b * N_E + i * NQ + 2 * n + 2)
                nc.vector.tensor_reduce(NM[:, m:m + 2], SP_[:, k:k + 2, 0:P * (i + 1)], AX.X, ALU.max,
                                        negate=True).then_inc(max_ready, 2)

            def diff(b, i, n):
                u = i * H + n
                gu = b * N_U + u
                w = P * (i + 1)
                e = 512 * (u % 2) if i < 4 else 0
                col = 8 * (n // 8) + 4 * (n % 2) + (n % 8) // 2
                after(dve, exp_done, 2 * gu + 2)
                nc.vector.reciprocal(RS[:, i % 2, :, col], SUM[:, i % 2, :, col]).then_inc(d_chain, 1)
                after(dve, d_chain, 2 * gu + 1)
                nc.vector.scalar_tensor_tensor(out=CC[:, u % 2:u % 2 + 1], in0=SUM[:, i % 2, 0, col:col + 1], scalar=neglam[:, 0:1],
                                               in1=RS[:, i % 2, 1, col:col + 1], op0=ALU.mult, op1=ALU.mult).then_inc(d_chain, 1)
                after(dve, d_chain, 2 * gu + 2)
                nc.vector.scalar_tensor_tensor(out=E1[:, u % 2, 0:w], in0=E2[:, e:e + w], scalar=CC[:, u % 2:u % 2 + 1],
                                               in1=E1[:, u % 2, 0:w], op0=ALU.mult, op1=ALU.add).then_inc(d_ready, 1)

            def dve_work(T):
                b, t, nb, nf = T.b, T.t, T.nb, T.nf
                for hs in range(HS_TILE):
                    s, h = divmod(hs, 2)
                    if T.attend:
                        if t >= 4:
                            row_max(b, t, s, h)
                        elif h == 0:
                            row_max_pair(b, t, s)
                    if h == 0 and T.before(s - 1):
                        diff(*T.before(s - 1))
                    if T.attend:
                        slot = X[:, (t + 1) % 4, :]
                        if hs == LN1_STATS:
                            after(dve, x_in[(t + 1) % 2], 16 * (b * (TILES // 2) + (t + 1) // 2) + 16)
                            variance(0, slot, nb)
                        if hs == LN1_ROWS:
                            after(dve, m_x2t, nf)
                            normalise(0, slot, nb, xn_ready)
                        if hs == Q_ROPE:
                            rope_mul(nb, T.next, 0)
                        if hs == KV_ROPE:
                            rope_mul(nb, T.next, 1, b + 1)
                        if hs == Q_REST:
                            rest(nb, 0)
                        if hs == K_REST:
                            rest(nb, 1)
                    if T.finish:
                        tok = TOK[:, :].rearrange("p (c d) -> p c d", d=DV)
                        x1 = X1[:, (t - 1) % 4, :]
                        if hs == AT_ROWS:
                            after(dve, m_at, nf + 1)
                            if T.attend:
                                after(dve, m_xt, nb + 1)
                            nc.vector.tensor_tensor(tok, M[:, :].rearrange("p (c d) -> p c d", d=DV),
                                                    RS[:, (t - 1) % 2, 0, :].unsqueeze(2).broadcast_to([P, H, DV]),
                                                    ALU.mult).then_inc(attn_ready, 1)
                        if hs == MEAN_SQ:
                            after(dve, sq_ready, nf + 1)
                            nc.vector.tensor_reduce(MS[:, :], SQ[:, :].rearrange("p (c d) -> p c d", d=DV), AX.X,
                                                    ALU.add).then_inc(ms_chain, 1)
                            after(dve, ms_chain, nf + 1)
                            nc.vector.tensor_scalar(VE[:, :], MS[:, :], 1.0 / DV, EPS, ALU.mult, ALU.add).then_inc(ms_ready, 1)
                        if hs == O_SUM:
                            after(dve, m_wo, nf + 1)
                            nc.vector.tensor_tensor(x1, M[:, :], X[:, (t - 1) % 4, :], ALU.add).then_inc(x1_ready, 1)
                        if hs == LN2_STATS:
                            after(dve, x1_ready, nf + 1)
                            variance(1, x1, nf)
                        if hs == LN2_ROWS:
                            after(dve, m_ant, nf + 1)
                            normalise(1, x1, nf, xn2_ready)
                        if hs == LN2_REST:
                            after(dve, x2h_ready, nf + 1)
                            c = slice(P * ((t - 1) % 2), P * ((t - 1) % 2) + P)
                            nc.vector.scalar_tensor_tensor(
                                out=X2L[:, :, c], in0=M[:, :].rearrange("p (k n) -> p k n", k=KD), scalar=XS,
                                in1=X2H[:, :, c], op0=ALU.mult, op1=ALU.subtract).then_inc(x2_ready, 1)
                    if T.w2 and hs in OUT_AT:
                        j = OUT_AT.index(hs)
                        after(dve, f2_ready, T.no + j + 1)
                        after(dve, o_out, 16 * (T.no + j))
                        nc.vector.scalar_tensor_tensor(out=OUT[:, :], in0=F[:, :], scalar=1.0 / HS,
                                                       in1=X1[:, (t + j) % 4, :], op0=ALU.mult,
                                                       op1=ALU.add).then_inc(o_sum, 1)

            dve.wait_ge(qkv_in, 16 * 4)
            nc.vector.tensor_scalar(WQKV[:, :, 0:D], WQKV[:, :, 0:D], DH ** -0.5, None, ALU.mult).then_inc(wq_scaled, 1)

            dve.wait_ge(x_in[0], 16)
            variance(0, X[:, 0, :], 0)
            normalise(0, X[:, 0, :], 0, xn_ready)
            rope_mul(0, 0, 0)
            rope_mul(0, 0, 1)
            rest(0, 0)
            rest(0, 1)

            for j, (w, q, arrived) in enumerate(((w1f, W1Q, w1_in), (w2f, W2Q, w2_in))):
                dve.wait_ge(arrived, 16)
                link(nc.vector.tensor_reduce(wsum[:, j, :], w.rearrange("p (a c) -> p a c", a=64), AX.X, ALU.add,
                                             apply_absolute_value=True))
                nc.vector.tensor_reduce(wtot[:, j:j + 1], wsum[:, j, :], AX.X, ALU.add).then_inc(abs_sum, 1)
                dve.wait_ge(abs_all, j + 1)
                link(nc.vector.tensor_scalar(thr[:, j, 0:1], (F, M)[j][:, 0:1], 1.0 / (D * FF), TERNARY_CUT, ALU.mult, ALU.mult))
                link(nc.vector.tensor_scalar(thr[:, j, 1:2], thr[:, j, 0:1], -1.0, None, ALU.mult))
                qf = q[:, :, :].rearrange("p a b -> p (a b)")
                for k in range(4):
                    c = slice(FF * k, FF * (k + 1))
                    link(nc.vector.tensor_scalar(cutt, w[:, c], thr[:, j, 1:2], None, ALU.is_le))
                    ins = nc.vector.scalar_tensor_tensor(out=qf[:, c], in0=w[:, c], scalar=thr[:, j, 0:1], in1=cutt,
                                                         op0=ALU.is_ge, op1=ALU.subtract, saturate=False)
                    if k < 3:
                        link(ins)
                    else:
                        ins.then_inc((w1_cut, ready)[j], 1)
                        dve.wait_ge((w1_cut, ready)[j], 1)
            dve.wait_ge(w_in, 16 * 11)
            link(nc.vector.tensor_tensor(lamp[:, :, :], lamt[:, 0:4:2, :], lamt[:, 1:4:2, :], ALU.mult))
            nc.vector.tensor_reduce(lams2[:, :], lamp[:, :, :], AX.X, ALU.add).then_inc(lam_prod, 1)
            dve.wait_ge(lam_exp, 1)
            link(nc.vector.tensor_tensor(lams2[:, 0:1], lame[:, 1:2], lame[:, 0:1], ALU.subtract))
            nc.vector.tensor_scalar(neglam[:, :], lams2[:, 0:1], -LAMBDA_INIT, None, ALU.add).then_inc(ready, 1)
            link(nc.vector.tensor_scalar(subc[:, :], subc[:, :], 1.0 - LAMBDA_INIT, None, ALU.mult))
            nc.vector.tensor_scalar(WO[:, :, :], WO[:, :, :], subc[:, 0:1], None, ALU.mult).then_inc(ready, 1)
            dve.wait_ge(ready, 3)
            every_block(dve, dve_work)

        @block.tensor
        def _(pe):
            pe.wait_ge(pool_const, 8)
            def transposes(src, n, done):
                for j in range(n):
                    ins = pe.transpose(M[:, P * j:P * (j + 1)], src[:, P * j:P * (j + 1)], ident[:, :])
                ins.then_inc(done, 1)

            def project(w, c0, js, done):
                for j in js:
                    ins = pe.matmul(M[:, :], WT[:, P * j:P * (j + 1)], w[:, j, c0:c0 + 512], start=(j == 0), stop=(j == KD - 1))
                if js[-1] == KD - 1:
                    ins.then_inc(done, 1)

            def scores(b, i, s):
                w = P * (i + 1)
                k = banks(i, s)
                if s == 0:
                    after(pe, stacked, 16 * 2 * PROD * (b * TILES + i + 1))
                after(pe, exp_done, b * N_E + SLOT_FREE[i * NQ + s])
                q = QST[0:ROWS, i % 2, (s % 8) * 4 + s // 8, :]
                kk = ((s // 2) % 8) * 2 + (s // 2) // 8
                for a in range(0, w, 512):
                    n = min(512, w - a)
                    last = a + n == w
                    pe.matmul(SP_[:, k[a // 512], 0:n], q, KST[0:ROWS, a // P:(a + n) // P, kk, :], start=True, stop=not last)
                ins = pe.matmul(SP_[:, k[(w - P) // 512], (w - P) % 512:(w - P) % 512 + P], identb[:, :], maskb[:, :],
                                start=False, stop=True)
                ins.then_inc(s_ready, 1)

            def diff_transposes(b, i, n, g):
                u = i * H + n
                t0 = b * N_T + tg(i, n, 0)
                after(pe, d_ready, b * N_U + u + 1)
                after(pe, dt_ready, t0 - 1 if g == 0 and n and groups(i) == 2 else t0)
                for k in range(4 * g, min(4 * g + 4, i + 1)):
                    ins = pe.transpose((DP, DX)[g][:, P * (k % 4):P * (k % 4 + 1)], E1[:, u % 2, P * k:P * (k + 1)], ident[:, :])
                ins.then_inc(t_ready, 1)

            def half_v(T, s, g):
                done = T.before(s - 2)
                if not done or done[2] % HALF != HALF - 1 or g >= groups(done[1]):
                    return
                b, i, n = done
                u = n // HALF
                after(pe, dt_ready, b * N_T + tg(i, n, g) + 1)
                if g == 0 and u == 0:
                    after(pe, rest_part, 2 * T.nb + 1)
                    if i == 0:
                        after(pe, v0_moved, b + 1)
                    else:
                        after(pe, kv_roped, b * TILES + i + 1)
                if g == 0 and u == 1:
                    after(pe, rest_part, 2 * T.nb)
                    after(pe, x2_ready, T.nf)
                for k in range(4 * g, min(4 * g + 4, i + 1)):
                    for q in range(4):
                        v = DV * (4 * u + q)
                        ins = pe.matmul(M[DV * q:DV * (q + 1), 0:2 * P], V[:, k, v:v + DV],
                                        DT[:, k, 2 * q:2 * q + 2, :], start=(k == 0), stop=(k == i), skip_group_check=True)
                ins.then_inc(pv_done, 1)

            def scores_ahead(T, s):
                if T.attend and s < H:
                    scores(T.b, T.t, 2 * s)
                    if T.t < 4:
                        scores(T.b, T.t, 2 * s + 1)

            def first_product(q, k, j):
                f = 2 * k + j
                if j == 0:
                    hold(pe, x2_ready, 2 * q + 2)
                    if k == 0:
                        hold(pe, o_sum, 2 * q)
                    else:
                        hold(pe, hp_ready, 8 * q + k)
                for c in range(KD):
                    for xp in (X2H, X2L):
                        ins = pe.matmul(F[:, 2 * P * j:2 * P * (j + 1)], W1Q[:, c, P * f:P * (f + 1)], xp[:, c, :],
                                        start=(c == 0 and xp is X2H), stop=(c == KD - 1 and xp is X2L))
                if j == 1:
                    ins.then_inc(f1_ready, 1)

            def second_product(q, j, fs):
                if fs[0] == 0:
                    hold(pe, h_ready, 8 * q + 8)
                    hold(pe, hp_ready, 8 * q + 8)
                    hold(pe, o_sum, 2 * q + j)
                for f in fs:
                    for hp in (HH, HL):
                        ins = pe.matmul(F[:, :], hp[:, f, P * j:P * (j + 1)], W2Q[:, f, :],
                                        start=(f == 0 and hp is HH), stop=(f == FT - 1 and hp is HL))
                if fs[-1] == FT - 1:
                    ins.then_inc(f2_ready, 1)

            def pe_work(T):
                b, t, nb, nf = T.b, T.t, T.nb, T.nf
                for hs in range(HS_TILE):
                    s, h = divmod(hs, 2)
                    if hs == 0:
                        scores_ahead(T, 0)
                    if h == 0 and T.attend and t >= 4:
                        scores(b, t, 2 * s + 1)
                    if h == 1:
                        if T.before(s - 1):
                            for g in range(groups(T.before(s - 1)[1])):
                                diff_transposes(*T.before(s - 1), g)
                        half_v(T, s, 1)
                    if T.attend and hs == LN1_TURN:
                        after(pe, xn_ready, nb + 1)
                        if T.finish:
                            after(pe, at_ready, 2 * nf + 2)
                        transposes(TOK, KD, m_xt)
                    if T.finish and hs == AT_TURN:
                        if T.attend:
                            after(pe, xt_ready, nb + 1)
                        after(pe, at_ready, 2 * nf + 2)
                        transposes(AT, KD, m_at)
                    if T.attend:
                        if hs == Q_PROJ[0]:
                            after(pe, xt_ready, nb + 1)
                            if T.finish:
                                after(pe, attn_ready, nf + 1)
                        if hs in Q_PROJ:
                            project(WQKV, 0, [j for j in range(KD) if Q_PROJ[j] == hs], m_q)
                        if hs == KV_PROJ[0]:
                            after(pe, q_roped, nb + 1)
                        if hs in KV_PROJ:
                            project(WQKV, D, [j for j in range(KD) if KV_PROJ[j] == hs], m_kv)
                        if hs == Q_TURN:
                            after(pe, kv_roped, nb + 1)
                            after(pe, rope_sum, 2 * nb + 1)
                            transposes(T1, KD, m_qt)
                        if hs == K_TURN:
                            after(pe, at_ready, 2 * nb - 1)
                            after(pe, rope_sum, 2 * nb + 2)
                            transposes(T1[:, D:D + DKV], 2, m_kt)
                    if T.finish:
                        if hs == AN_TURN:
                            if T.attend:
                                after(pe, rest_part, 2 * nb + 2)
                            after(pe, an_ready, nf + 1)
                            transposes(TOK, KD, m_ant)
                        if hs == O_PROJ[0]:
                            after(pe, ant_ready, nf + 1)
                        if hs in O_PROJ:
                            project(WO, 0, [j for j in range(KD) if O_PROJ[j] == hs], m_wo)
                        if hs == LN2_TURN:
                            after(pe, x1_ready, nf + 1)
                            after(pe, xn2_ready, nf + 1)
                            transposes(TOK, KD, m_x2t)
                    piece = T.first_product(hs)
                    if piece and piece[1] < 2:
                        first_product(T.pair, *piece)
                    if T.second_product(hs):
                        second_product(T.pair, *T.second_product(hs))
                    if h == 0:
                        scores_ahead(T, s + 1)
                        half_v(T, s, 0)

            pe.wait_ge(xn_ready, 1)
            transposes(TOK, KD, m_xt)
            pe.wait_ge(xt_ready, 1)
            pe.wait_ge(wq_scaled, 1)
            project(WQKV, 0, range(KD), m_q)
            pe.wait_ge(q_roped, 1)
            project(WQKV, D, range(KD), m_kv)
            pe.wait_ge(kv_roped, 1)
            pe.wait_ge(rope_sum, 1)
            transposes(T1, KD, m_qt)
            pe.wait_ge(rest_part, 1)
            pe.wait_ge(rope_sum, 2)
            transposes(T1[:, D:D + DKV], 2, m_kt)
            for j in range(2):
                after(pe, abs_sum, j + 1)
                pe.matmul((F, M)[j][:, 0:1], onesf, wtot[:, j:j + 1], start=True, stop=True).then_inc(abs_all, 1)
            pe.wait_ge(ready, 3)
            every_block(pe, pe_work)


def rope_tables():
    inv = (np.float32(ROPE_THETA) ** (-np.arange(DH, dtype=np.float32) / np.float32(DH))).astype(np.float32)
    f = (np.arange(S, dtype=np.float32)[:, None] * inv[None, :]).astype(np.float32)
    cos, sin = np.cos(f).astype(np.float32), np.sin(f).astype(np.float32)
    sin[:, :DH // 2] *= -1
    t = np.stack([cos, sin])
    return np.ascontiguousarray(t.reshape(2, TILES, P, DH).transpose(2, 0, 1, 3))


def kernel(**inputs):
    import numpy as _np
    import concourse.bacc as _bacc
    from concourse import mybir as _mybir
    from concourse.bass_utils import run_bass_kernel_spmd as _run

    nc = _bacc.Bacc("TRN2", target_bir_lowering=False, num_devices=1)
    a = {k: _np.asarray(v) for k, v in inputs.items()}
    x = a["L0_attn_hidden_states"]
    arrays = {
        "x": _np.concatenate([x, x[:1]], axis=0),
        "wqT": a["L0_attn_Wq"].T, "wkT": a["L0_attn_Wk"].T, "wvT": a["L0_attn_Wv"].T,
        "woT": a["L0_attn_Wo"].T.reshape(2, 4, 2, DV, D).transpose(0, 2, 1, 3, 4).reshape(KD, P, D),
        "lams": _np.stack([a["L0_attn_lambda_q1"], a["L0_attn_lambda_k1"], a["L0_attn_lambda_q2"], a["L0_attn_lambda_k2"]]),
        "subw": a["L0_attn_subln_weight"],
        "w1T": a["L0_ffn_w1"].T, "b1": a["L0_ffn_b1"].reshape(FT, P).T,
        "w2T": a["L0_ffn_w2"].T, "b2": a["L0_ffn_b2"],
        "rope": rope_tables(),
    }
    feeds, args = {}, []
    for name, v in arrays.items():
        v = _np.ascontiguousarray(v)
        feeds[f"in_{name}"] = v
        args.append(nc.dram_tensor(f"in_{name}", v.shape, _mybir.dt.from_np(v.dtype), kind="ExternalInput").ap())
    args.append(nc.dram_tensor("out_0", (B, S, D), F32, kind="ExternalOutput").ap())
    diff_attention_ffn(nc, *args)
    r = _run(nc, [feeds], core_ids=[0])
    return r.results[0]["out_0"]
```
